# Optimizing a Trainium2 kernel written in Bass

```python
import numpy as np
import jax
import jax.numpy as jnp

def _softmax(x, axis=-1):
    return jax.nn.softmax(x, axis=axis)

def _gelu(x):
    return jax.nn.gelu(x, approximate=True)

def _silu(x):
    return jax.nn.silu(x)

def _sigmoid(x):
    return jax.nn.sigmoid(x)

def _layernorm(x, axis=-1, eps=1e-05):
    m = jnp.mean(x, axis=axis, keepdims=True)
    v = jnp.var(x, axis=axis, keepdims=True)
    return (x - m) / jnp.sqrt(v + eps)

def _scatter_add(tgt, idx, src, axis=0):
    return tgt.at[idx].add(src)

def _segment_sum(src, seg, n):
    return jax.ops.segment_sum(src, seg, n)
kernel_name = 'mk_adj_resnorm_d4_adj_r2_c8d3b8'

def setup_inputs(seed: int=0):
    np.random.seed(seed)
    _w = jnp.asarray

    def _rec_inputs():
        import jax
        import jax.numpy as jnp
        _gk = jax.random.key(seed)
        x = -0.000929 + 1 * jax.random.normal(jax.random.fold_in(_gk, 1), (8192, 64), jnp.float32)
        _w = (1.0 + jnp.arange(8192, dtype=jnp.float32)) ** (-0.5)
        _w = _w / _w.mean()
        _pij = jnp.clip(0.00195312 * _w[:, None] * _w[None, :], 0.0, 1.0)
        _a = jax.random.uniform(jax.random.fold_in(_gk, 2), (8192, 8192)) < _pij
        _a = jnp.logical_or(_a, jnp.eye(8192, dtype=bool))
        _af = _a.astype(jnp.float32)
        _af = _af * jax.random.uniform(jax.random.fold_in(_gk, 3), (8192, 8192), jnp.float32, 0.05, 1)
        adj = _af
        return (x, adj)
    x, adj = _rec_inputs()

    def _L0_gnn_setup():
        import jax, jax.numpy as jnp
        import numpy as np
        N = 8192
        IN_C = 64
        OUT_C = 64
        key = jax.random.key(seed)
        k1, k2, k3 = jax.random.split(key, 3)
        g_data = jax.random.normal(k1, (N, IN_C), dtype=jnp.float32)
        g_adj = jax.random.uniform(k2, (N, N), dtype=jnp.float32)
        bound = 1.44 * np.sqrt(6.0 / (IN_C + OUT_C))
        W = jax.random.uniform(k3, (IN_C, OUT_C), dtype=jnp.float32, minval=-bound, maxval=bound)
        return {'g_data': g_data, 'g_adj': g_adj, 'W': W}
    _L0_gnn_all = _L0_gnn_setup()
    _L0_gnn_in = {k: v for k, v in _L0_gnn_all.items() if k in ('W',)}
    del _L0_gnn_all

    def _L1_gnn_setup():
        import jax, jax.numpy as jnp
        import numpy as np
        N = 5000
        DIM = 64
        F_CONST = 1.0
        B_CONST = 0.1
        R_CONST = 0.01
        key = jax.random.key(seed)
        k1, k2 = jax.random.split(key)
        t = jnp.zeros((1,), dtype=jnp.float32)
        x = jax.random.uniform(k1, (N, DIM), dtype=jnp.float32)
        A = jax.random.uniform(k2, (N, N), dtype=jnp.float32)
        return {'t': t, 'x': x, 'A': A}
    _L1_gnn_all = _L1_gnn_setup()
    _L1_gnn_in = {k: v for k, v in _L1_gnn_all.items() if k in ('t',)}
    del _L1_gnn_all

    def _L2_gnn_setup():
        import jax, jax.numpy as jnp
        import numpy as np
        N = 8192
        INFEAT = 64
        OUTFEAT = 64
        EPS = 1e-07
        key = jax.random.key(seed)
        k1, k2, k3, k4 = jax.random.split(key, 4)
        x = jax.random.normal(k1, (N, INFEAT), dtype=jnp.float32)
        adj = jax.random.uniform(k2, (N, N), dtype=jnp.float32)
        limit = float(np.sqrt(6.0 / (INFEAT + OUTFEAT)))
        W_weight = jax.random.uniform(k3, (OUTFEAT, INFEAT), dtype=jnp.float32, minval=-limit, maxval=limit)
        W_bias = jax.random.normal(k4, (OUTFEAT,), dtype=jnp.float32) * 0.01
        return {'x': x, 'adj': adj, 'W_weight': W_weight, 'W_bias': W_bias}
    _L2_gnn_all = _L2_gnn_setup()
    _L2_gnn_in = {k: v for k, v in _L2_gnn_all.items() if k in ('W_weight', 'W_bias')}
    del _L2_gnn_all

    def _L3_gnn_setup():
        import jax, jax.numpy as jnp
        import numpy as np
        N = 4096
        H = 64
        ALPHA = 0.2
        NEG_INF = -9000000000000000.0

        def gru_cell(x, h, w_ih, w_hh, b_ih, b_hh):
            gi = x @ w_ih.T + b_ih
            gh = h @ w_hh.T + b_hh
            ir, iz, inn = jnp.split(gi, 3, axis=1)
            hr, hz, hn = jnp.split(gh, 3, axis=1)
            r = jax.nn.sigmoid(ir + hr)
            z = jax.nn.sigmoid(iz + hz)
            n = jnp.tanh(inn + r * hn)
            return (1.0 - z) * n + z * h

        def gat(h, node_adj, edge_adj, W, a):
            hw = h @ W
            h_plus = (node_adj > 0).astype(hw.dtype) @ hw
            h_minus = (node_adj < 0).astype(hw.dtype) @ hw
            e_plus = jax.nn.leaky_relu(jnp.concatenate([h_plus, h_minus], axis=1) @ a, ALPHA)
            e_minus = jax.nn.leaky_relu(jnp.concatenate([h_minus, h_plus], axis=1) @ a, ALPHA)
            att = jnp.where(edge_adj > 0, e_plus, NEG_INF)
            att = jnp.where(edge_adj < 0, e_minus, att)
            att = jax.nn.softmax(att, axis=1)
            return att * edge_adj @ hw
        key = jax.random.key(seed)
        ks = jax.random.split(key, 12)
        f32 = jnp.float32
        inp = {'h': jax.random.normal(ks[0], (N, H), f32), 'node_adj': jax.random.normal(ks[1], (N, N), f32), 'edge_adj': jax.random.normal(ks[2], (N, N), f32), 'W_gat': jax.random.normal(ks[3], (H, H), f32) * (1.414 * np.sqrt(6.0 / (2 * H))), 'a_gat': jax.random.normal(ks[4], (2 * H, 1), f32) * (1.414 * np.sqrt(6.0 / (2 * H + 1))), 'w_ih_e': jax.random.normal(ks[5], (3 * H, 2 * H), f32) * 0.01, 'w_hh_e': jax.random.normal(ks[6], (3 * H, H), f32) * 0.01, 'b_ih_e': jnp.zeros((3 * H,), f32), 'b_hh_e': jnp.zeros((3 * H,), f32), 'w_ih_n': jax.random.normal(ks[7], (3 * H, H), f32) * 0.01, 'w_hh_n': jax.random.normal(ks[8], (3 * H, H), f32) * 0.01, 'b_ih_n': jnp.zeros((3 * H,), f32), 'b_hh_n': jnp.zeros((3 * H,), f32)}
        return inp
    _L3_gnn_all = _L3_gnn_setup()
    _L3_gnn_in = {k: v for k, v in _L3_gnn_all.items() if k in ('W_gat', 'a_gat', 'w_ih_e', 'w_hh_e', 'b_ih_e', 'b_hh_e', 'w_ih_n', 'w_hh_n', 'b_ih_n', 'b_hh_n')}
    del _L3_gnn_all
    return {'x': x, 'adj': adj, 'L0_gnn_W': _L0_gnn_in['W'], 'L1_gnn_t': _L1_gnn_in['t'], 'L2_gnn_W_weight': _L2_gnn_in['W_weight'], 'L2_gnn_W_bias': _L2_gnn_in['W_bias'], 'L3_gnn_W_gat': _L3_gnn_in['W_gat'], 'L3_gnn_a_gat': _L3_gnn_in['a_gat'], 'L3_gnn_w_ih_e': _L3_gnn_in['w_ih_e'], 'L3_gnn_w_hh_e': _L3_gnn_in['w_hh_e'], 'L3_gnn_b_ih_e': _L3_gnn_in['b_ih_e'], 'L3_gnn_b_hh_e': _L3_gnn_in['b_hh_e'], 'L3_gnn_w_ih_n': _L3_gnn_in['w_ih_n'], 'L3_gnn_w_hh_n': _L3_gnn_in['w_hh_n'], 'L3_gnn_b_ih_n': _L3_gnn_in['b_ih_n'], 'L3_gnn_b_hh_n': _L3_gnn_in['b_hh_n']}

def reference(x, adj, L0_gnn_W, L1_gnn_t, L2_gnn_W_weight, L2_gnn_W_bias, L3_gnn_W_gat, L3_gnn_a_gat, L3_gnn_w_ih_e, L3_gnn_w_hh_e, L3_gnn_b_ih_e, L3_gnn_b_hh_e, L3_gnn_w_ih_n, L3_gnn_w_hh_n, L3_gnn_b_ih_n, L3_gnn_b_hh_n):
    import jax
    import jax.numpy as jnp

    def _L0_gnn_ref(g_data, g_adj, W):
        import jax, jax.numpy as jnp
        import numpy as np
        N = 8192
        IN_C = 64
        OUT_C = 64
        n = g_adj.shape[0]
        a = g_adj + jnp.eye(n, dtype=g_adj.dtype)
        deg = a.sum(axis=1)
        dinv = jnp.where(deg > 0, deg ** (-0.5), 0.0)
        a_norm = dinv[:, None] * a * dinv[None, :]
        out = a_norm @ g_data
        out = out @ W
        return out

    def _L1_gnn_ref(t, x, A):
        import jax, jax.numpy as jnp
        import numpy as np
        N = 5000
        DIM = 64
        F_CONST = 1.0
        B_CONST = 0.1
        R_CONST = 0.01
        Ax = A @ x
        outer = R_CONST * jnp.sum(x * Ax, axis=1, keepdims=True)
        return F_CONST - B_CONST * x - outer

    def _L2_gnn_ref(x, adj, W_weight, W_bias):
        import jax, jax.numpy as jnp
        import numpy as np
        N = 8192
        INFEAT = 64
        OUTFEAT = 64
        EPS = 1e-07
        n = adj.shape[0]
        idx = jnp.arange(n)
        adj_sl = adj.at[idx, idx].add(1.0)
        h_k_N = adj_sl @ x
        h_k = jax.nn.relu(h_k_N @ W_weight.T + W_bias)
        norm = jnp.linalg.norm(h_k, axis=1, keepdims=True)
        return h_k / (norm + EPS)

    def _L3_gnn_ref(h, node_adj, edge_adj, W_gat, a_gat, w_ih_e, w_hh_e, b_ih_e, b_hh_e, w_ih_n, w_hh_n, b_ih_n, b_hh_n):
        import jax, jax.numpy as jnp
        import numpy as np
        N = 4096
        H = 64
        ALPHA = 0.2
        NEG_INF = -9000000000000000.0

        def gru_cell(x, h, w_ih, w_hh, b_ih, b_hh):
            gi = x @ w_ih.T + b_ih
            gh = h @ w_hh.T + b_hh
            ir, iz, inn = jnp.split(gi, 3, axis=1)
            hr, hz, hn = jnp.split(gh, 3, axis=1)
            r = jax.nn.sigmoid(ir + hr)
            z = jax.nn.sigmoid(iz + hz)
            n = jnp.tanh(inn + r * hn)
            return (1.0 - z) * n + z * h

        def gat(h, node_adj, edge_adj, W, a):
            hw = h @ W
            h_plus = (node_adj > 0).astype(hw.dtype) @ hw
            h_minus = (node_adj < 0).astype(hw.dtype) @ hw
            e_plus = jax.nn.leaky_relu(jnp.concatenate([h_plus, h_minus], axis=1) @ a, ALPHA)
            e_minus = jax.nn.leaky_relu(jnp.concatenate([h_minus, h_plus], axis=1) @ a, ALPHA)
            att = jnp.where(edge_adj > 0, e_plus, NEG_INF)
            att = jnp.where(edge_adj < 0, e_minus, att)
            att = jax.nn.softmax(att, axis=1)
            return att * edge_adj @ hw
        d_node = jnp.diag(node_adj)
        d_edge = jnp.diag(edge_adj)
        A_node = node_adj - jnp.diag(d_node)
        A_edge = edge_adj - jnp.diag(d_edge)
        node_support = jnp.concatenate([(A_node > 0).astype(h.dtype) @ h, (A_node < 0).astype(h.dtype) @ h], axis=1)
        edge_output = gru_cell(node_support, h, w_ih_e, w_hh_e, b_ih_e, b_hh_e)
        edge_support = gat(h, A_node, A_edge, W_gat, a_gat)
        node_output = gru_cell(edge_support, h, w_ih_n, w_hh_n, b_ih_n, b_hh_n)
        return d_edge[:, None] * edge_output + d_node[:, None] * node_output
    x = _layernorm(x + _L0_gnn_ref(x, adj, L0_gnn_W), axis=-1)
    x = _layernorm(x + _L1_gnn_ref(L1_gnn_t, x, adj), axis=-1)
    x = _layernorm(x + _L2_gnn_ref(x, adj, L2_gnn_W_weight, L2_gnn_W_bias), axis=-1)
    x = _layernorm(x + _L3_gnn_ref(x, adj, adj, L3_gnn_W_gat, L3_gnn_a_gat, L3_gnn_w_ih_e, L3_gnn_w_hh_e, L3_gnn_b_ih_e, L3_gnn_b_hh_e, L3_gnn_w_ih_n, L3_gnn_w_hh_n, L3_gnn_b_ih_n, L3_gnn_b_hh_n), axis=-1)
    return x

_drawn_inputs = setup_inputs


def setup_inputs(seed=0):
    import zlib

    import numpy as np

    out = dict(_drawn_inputs(seed))
    spreads = {'L3_gnn_b_ih_e': (0.0, 0.441),
     'L3_gnn_b_hh_e': (0.0, 0.709),
     'L3_gnn_b_ih_n': (0.0, 0.368),
     'L3_gnn_b_hh_n': (0.0, 0.773)}
    factors = {'L2_gnn_W_bias': 64.0,
     'L3_gnn_W_gat': 8.0,
     'L3_gnn_w_hh_e': 6.051,
     'L3_gnn_w_ih_n': 8.0,
     'L3_gnn_w_hh_n': 6.085}
    for name, (base, spread) in spreads.items():
        noise = np.random.default_rng([zlib.crc32(name.encode()), seed]).standard_normal(out[name].shape)
        drawn = base * np.exp(spread * noise) if base else spread * noise
        out[name] = jnp.asarray(drawn.astype(out[name].dtype))
    for name, factor in factors.items():
        out[name] = (out[name] * factor).astype(out[name].dtype)
    return out
```

```python
from contextlib import ExitStack

import concourse.bass as bass
from concourse import mybir

F32 = mybir.dt.float32
BF16 = mybir.dt.bfloat16
F16 = mybir.dt.float16
I32 = mybir.dt.int32
ALU = mybir.AluOpType
ACT = mybir.ActivationFunctionType
AX = mybir.AxisListType

P = 128
N = 8192
D = 64
ROWS = 8
SB = N // ROWS
Q = 4
KK = SB // P // Q
G = SB // P
TILES = N // P
HALF = 512
H_SCALE = 4096.0
L_SCALE = 2048.0
CQ = 32
LN_EPS = 1e-5
NORM_EPS = 1e-7
NEG_INF = -9000000000000000.0
SLOPE = 0.2


class RingSems:
    pass


def build(nc, adj, x_in, w0, w2t, b2, wg, wgt, a_gat, wihe, whhe, bihe, bhhe, wihn, whhn, bihn, bhhn, out):
    ctx = ExitStack()
    with ctx:
        def sb(name, shape, dt=F32):
            return ctx.enter_context(nc.sbuf_tensor(name, shape, dt))

        def pb(name, shape):
            return ctx.enter_context(nc.psum_tensor(name, shape, F32))

        def sem(name):
            return ctx.enter_context(nc.semaphore(name))

        X = sb("X", [P, TILES, 2 * D])
        H = sb("H", [P, TILES, 2 * D], F16)
        part = sb("part", [P, TILES, D])
        sign_part = sb("sign_part", [P, TILES, D + 1])
        neg_part = sb("neg_part", [P, TILES, D + 1])
        dinv = sb("dinv", [P, TILES])
        diag = sb("diag", [P, TILES])
        ring = sb("ring", [P, Q, KK, SB])
        signs = sb("signs", [P, Q, KK, SB], F16)
        xs = sb("xs", [P, Q, KK, 2 * D])
        hs = sb("hs", [P, Q, KK, 2 * D], F16)
        sums_sb = sb("sums_sb", [P, SB])
        aux_sb = sb("aux_sb", [P, SB])
        sign_sb = sb("sign_sb", [P, SB])
        degree_acc = sb("degree_acc", [P, KK, SB])
        count_sb = {4: degree_acc[:, 0, :], 5: aux_sb[:, :]}
        unused = signs[:, 0:1, :, :].rearrange("p q k i -> p (q k i)")
        v = sb("v", [P, G, D])
        w = sb("w", [P, G, D])
        z = sb("z", [P, G, D])
        stat = [sb(f"stat{n}", [P, G]) for n in range(4)]
        root_in = sb("root_in", [P, G])
        root_out = sb("root_out", [P, G])
        neg_sum = sb("neg_sum", [P, 1])
        any_neg = sb("any_neg", [1, 1], I32)
        ident = sb("ident", [P, P])
        off_diag = sb("off_diag", [P, P])
        ones = sb("ones", [P, 1])
        both = {s: sb(f"both{s}", [P, P]) for s in (2, 3, 4)}
        fold_w0 = sb("fold_w0", [P, D])
        fold_id = sb("fold_id", [P, D])
        fold_h = sb("fold_h", [P, D])
        fold_count = sb("fold_count", [P, 1])
        fold_w2 = sb("fold_w2", [P, D])
        fold_wg = sb("fold_wg", [P, D])
        fold = {1: fold_w0[:, :], 2: fold_w0[:, :], 3: fold_id[:, :], 4: fold_w2[:, :], 5: fold_wg[:, :]}
        b2_sb = sb("b2_sb", [P, D])
        wgt_sb = sb("wgt_sb", [D, D])
        a_sb = sb("a_sb", [D, 2])
        score_w = sb("score_w", [P, 2])
        w_edge = sb("w_edge", [P, 4 * D])
        w_rest = sb("w_rest", [P, 8 * D])
        gate_b16 = sb("gate_b16", [2 * CQ + 2, 8 * D], BF16)
        ones16 = sb("ones16", [P, P], BF16)
        ones_h = sb("ones_h", [P, CQ], F16)

        sums = pb("sums", [P, SB])
        sign_sums = pb("sign_sums", [P, SB])
        counts = pb("counts", [P, SB])
        turn = pb("turn", [P, SB])
        turned = turn[:, :].rearrange("p (g c) -> p g c", g=G)
        sign_turned = counts[:, :].rearrange("p (g c) -> p g c", g=G)

        S = sb("S", [P, G, 2 * D])
        ST = sb("ST", [P, G, P])
        ET = sb("ET", [P, G, P])
        rz = sb("rz", [P, G, 2, 2 * D])
        EH = rz[:, 0:G // 2, :, :].rearrange("p g n c -> p (g n) c")
        cand = degree_acc[:, :, :].rearrange("p k (g c) -> p (k g) c", c=4 * D)
        cand = cand.rearrange("p g (n c) -> p g n c", n=2)
        RP = z[:, :, :]
        early = S[:, :, :].rearrange("p g c -> p (g c)")
        gate_b = early[0:2 * CQ + 2, 0:8 * D]
        gate_b_rest = early[0:2 * CQ + 2, 8 * D:16 * D]
        bias16 = ST[0:2 * CQ + 2, 0:2, :].rearrange("p g c -> p (g c)").bitcast(BF16)
        neg_seen = ET[:, 0:2, :].rearrange("p g c -> p (g c)")
        cnt = sb("cnt", [P, 3, G])
        ee = sb("ee", [P, 4, G])
        ex = sb("ex", [P, 3, G])
        fs = sb("fs", [P, 3, G])
        final_in = sb("final_in", [P, G])
        final_root = sb("final_root", [P, G])

        def ring_sems(of):
            k = RingSems()
            k.loaded = [sem(f"{of}loaded{q}") for q in range(Q)]
            k.used = sem(f"{of}used")
            k.masked = sem(f"{of}masked")
            k.signs_used = sem(f"{of}signs_used")
            k.staged = sem(f"{of}staged")
            k.h_staged = sem(f"{of}h_staged")
            k.act_copied = sem(f"{of}act_copied")
            k.dve_copied = sem(f"{of}dve_copied")
            k.t_ready = sem(f"{of}t_ready")
            k.t_free = sem(f"{of}t_free")
            k.s_ready = sem(f"{of}s_ready")
            k.s_free = sem(f"{of}s_free")
            return k

        main = ring_sems("")
        extra = ring_sems("extra_")
        loaded, used, masked, signs_used = main.loaded, main.used, main.masked, main.signs_used
        staged, h_staged = main.staged, main.h_staged
        act_copied, dve_copied, t_ready, t_free, s_ready, s_free = (
            main.act_copied, main.dve_copied, main.t_ready, main.t_free, main.s_ready, main.s_free)
        x_loaded = sem("x_loaded")
        weights_loaded = sem("weights_loaded")
        zeroed = sem("zeroed")
        ident_made = sem("ident_made")
        rhs_made = sem("rhs_made")
        summed = sem("summed")
        scanned = sem("scanned")
        diag_ready = sem("diag_ready")
        x_done = sem("x_done")
        root_asked = sem("root_asked")
        root_given = sem("root_given")
        neg_summed = sem("neg_summed")
        flag_ready = sem("flag_ready")
        score_made = sem("score_made")
        score_copied = sem("score_copied")
        s_built = sem("s_built")
        st_made = sem("st_made")
        st_copied = sem("st_copied")
        e_made = sem("e_made")
        e_shifted = sem("e_shifted")
        exp_made = sem("exp_made")
        eh_built = sem("eh_built")
        et_made = sem("et_made")
        et_copied = sem("et_copied")
        gates_made = sem("gates_made")
        gates_read = sem("gates_read")
        cand_ready = sem("cand_ready")
        cand_made = sem("cand_made")
        var_ready = sem("var_ready")
        std_made = sem("std_made")
        y_ready = sem("y_ready")
        stored = sem("stored")
        passed = {nc.gpsimd: sem("pool_passed"), nc.sync: sem("sp_passed"), nc.vector: sem("dve_passed")}

        PAIRS = ROWS * (ROWS - 1) // 2
        TRI = PAIRS + ROWS
        SEEN0 = {1: 0, 2: PAIRS, 3: PAIRS + TRI, 4: PAIRS + 2 * TRI, 5: PAIRS + 3 * TRI}
        T0 = {2: 2 * ROWS, 3: 3 * ROWS, 4: 4 * ROWS, 5: 5 * ROWS}
        ACT0 = {1: 0, 2: ROWS - 1, 3: 2 * (ROWS - 1), 4: 3 * (ROWS - 1), 5: 4 * (ROWS - 1)}
        DVE0 = {2: 0, 3: ROWS, 4: 2 * ROWS, 5: 3 * ROWS}
        DIAG0 = {2: 0, 4: Q * ROWS, 5: 2 * Q * ROWS}
        SIGN0 = {4: 0, 5: PAIRS}
        SROW0 = {4: 0, 5: ROWS - 1}
        ALL = ROWS * ROWS
        LAYERS = {2: (0, 1), 3: (1, 0), 4: (0, 1)}

        def offs_before(r):
            return r * (r - 1) // 2

        def all_before(r):
            return r * (r + 1) // 2

        def row_of(s, r):
            return (ROWS - 1) - r if s in (2, 4) else r

        def grid(row, col):
            return (row * ROWS + col) * Q

        def for_rows(e, body):
            body(0)
            body(1)
            with e.Fori(2, ROWS) as r:
                body(r)

        def for_offs(e, r, body):
            if isinstance(r, int) and r == 0:
                return
            body(0)
            if not (isinstance(r, int) and r == 1):
                with e.Fori(1, r) as j:
                    body(j)

        def settle(e):
            e.sem_inc(passed[e], 1)

        def tiles(row):
            return bass.ds(row * G, G)

        block = ctx.enter_context(nc.Block())

        @block.sync
        def _(sp):
            sp.dma_start(X[:, :, D:2 * D], x_in.rearrange("p (t c) -> p t c", t=TILES)).then_inc(x_loaded, 16)

            def load(place, q, loaded=main.loaded):
                sp.dma_start(ring[:, q, :, :],
                             adj[bass.ds(place + q, 1)].rearrange("o p (k i) -> p (o k) i", k=KK)).then_inc(loaded[q], 16)

            def wait(semaphore, n):
                sp.wait_ge(semaphore, n)
                settle(sp)

            def row1(r):
                before = offs_before(r)
                with sp.Fori(r, ROWS) as k:
                    for q in range(Q):
                        wait(used, before * Q + q + 1)
                        wait(summed, (r * (ROWS - 1) + k) * Q + q + 1)
                        wait(scanned, (r * (ROWS - 1) + k) * Q + q + 1)
                        load(grid(r, k), q)

                def off(j):
                    for q in range(Q):
                        wait(used, (before + j) * Q + q + 1)
                        wait(summed, (r * (ROWS - 1) + ROWS + j) * Q + q + 1)
                        wait(scanned, (r * (ROWS - 1) + ROWS + j) * Q + q + 1)
                        load(grid(r, j), q)
                for_offs(sp, r, off)
            for_rows(sp, row1)
            sp.wait_ge(summed, ROWS * ROWS * Q + 4)
            sp.wait_ge(scanned, ROWS * ROWS * Q + 4)

            def row(s, r):
                before = SEEN0[s] + all_before(r)
                here = row_of(s, r)

                def one(n, place, signs_before):
                    for q in range(Q):
                        wait(used, (before + n) * Q + q + 1)
                        if signs_before is not None:
                            wait(masked, signs_before * Q + q + 1)
                        load(place, q)

                def signs_at(j):
                    return {4: offs_before(r) + j, 5: SIGN0[5] + all_before(r) + j}.get(s)
                for_offs(sp, r, lambda j: one(j, grid(here, row_of(s, j)), signs_at(j)))
                one(r, grid(here, here), signs_at(r))

            for s in (2, 3, 4):
                for_rows(sp, lambda r: row(s, r))

            sp.wait_ge(flag_ready, 1)
            flag = sp.value_load(any_neg[0:1, 0:1], min_val=0, max_val=1)
            with sp.If(flag > 0):
                sp.wait_ge(used, SEEN0[5] * Q + Q)
                sp.wait_ge(masked, SIGN0[5] * Q + Q)
                with sp.Fori(0, ROWS) as m:
                    with sp.Fori(0, ROWS) as j:
                        for q in range(Q):
                            wait(extra.used, (m * ROWS + j) * Q + q + 1)
                            wait(extra.masked, (m * ROWS + j) * Q + q + 1)
                            load(grid(m, (m + j) % ROWS), q, extra.loaded)
                sp.wait_ge(extra.used, ALL * Q + Q)
                sp.wait_ge(extra.masked, ALL * Q + Q)

            for_rows(sp, lambda r: row(5, r))
            with sp.Fori(0, ROWS) as f:
                wait(y_ready, f + 1)
                sp.dma_start(out.rearrange("p (t c) -> p t c", t=TILES)[:, tiles(f), :],
                             X[:, tiles(f), 0:D]).then_inc(stored, 16)
            sp.wait_ge(stored, 16 * ROWS)
        @block.gpsimd
        def _(pool):
            nc.gpsimd.memset(ident[:, :], 0.0)
            nc.gpsimd.memset(off_diag[:, :], 1.0)
            nc.gpsimd.memset(ones[:, :], 1.0)
            nc.gpsimd.memset(ones16[:, :], 1.0)
            nc.gpsimd.memset(ones_h[:, :], 1.0)
            for t in [both[s][:, :] for s in (2, 3, 4)] + [fold_count[:, :], w_edge[:, :], w_rest[:, :], gate_b, gate_b16[:, :]]:
                nc.gpsimd.memset(t, 0.0)
            nc.gpsimd.memset(neg_part[:, :, :], 0.0).then_inc(zeroed, 1)
            pool.wait_ge(zeroed, 1)
            nc.gpsimd.affine_select(out=ident[:, :], in_=ident[:, :], compare_op=ALU.not_equal, fill=1.0,
                                    base=0, pattern=[[-1, P]], channel_multiplier=1).then_inc(ident_made, 1)
            nc.gpsimd.affine_select(out=off_diag[:, :], in_=off_diag[:, :], compare_op=ALU.not_equal, fill=0.0,
                                    base=0, pattern=[[-1, P]], channel_multiplier=1).then_inc(ident_made, 1)
            pool.wait_ge(ident_made, 2)
            hi = ident[D:P, D:P]
            nc.gpsimd.tensor_copy(both[2][D:P, D:P], hi)
            nc.gpsimd.tensor_copy(both[3][D:P, 0:D], hi)
            nc.gpsimd.tensor_copy(fold_id[0:D, 0:D], ident[0:D, 0:D])
            nc.gpsimd.tensor_copy(fold_id[D:P, 0:D], hi)
            nc.gpsimd.tensor_scalar(fold_h[0:D, :], ident[0:D, 0:D], 1.0 / H_SCALE, None, ALU.mult)
            nc.gpsimd.tensor_scalar(fold_h[D:P, :], hi, 1.0 / (H_SCALE * L_SCALE), None, ALU.mult).then_inc(rhs_made, 1)
            pool.wait_ge(rhs_made, 1)
            for c in range(0, P, CQ):
                last = nc.gpsimd.memset(fold_count[c:c + 1, :], 1.0)
            last.then_inc(rhs_made, 1)

            loads = [
                (both[2][0:D, 0:D], w0), (both[3][0:D, D:P], w2t), (both[4][0:D, 0:D], w2t), (both[4][D:P, D:P], wg),
                (fold_w0[0:D, :], w0), (fold_w0[D:P, :], w0), (fold_w2[0:D, :], w2t), (fold_w2[D:P, :], w2t),
                (fold_wg[0:D, :], wg), (fold_wg[D:P, :], wg), (wgt_sb[:, :], wgt),
                (b2_sb[:, :], b2.partition_broadcast(P)),
                (a_sb[:, 0:1], a_gat[0:D, :]), (a_sb[:, 1:2], a_gat[D:2 * D, :]),
                (w_edge[:, 0:3 * D], wihe),
                (w_rest[D:P, 0:2 * D], whhe[:, 0:2 * D]), (w_rest[D:P, 3 * D:4 * D], whhe[:, 2 * D:3 * D]),
                (w_rest[0:D, 4 * D:7 * D], wihn),
                (w_rest[D:P, 4 * D:6 * D], whhn[:, 0:2 * D]), (w_rest[D:P, 7 * D:8 * D], whhn[:, 2 * D:3 * D]),
            ]
            for p in (0, CQ, 2 * CQ):
                loads += [
                    (gate_b[p:p + 1, 0:3 * D], bihe), (gate_b[p:p + 1, 4 * D:7 * D], bihn),
                    (gate_b[p + 1:p + 2, 0:2 * D], bhhe[:, 0:2 * D]), (gate_b[p + 1:p + 2, 3 * D:4 * D], bhhe[:, 2 * D:3 * D]),
                    (gate_b[p + 1:p + 2, 4 * D:6 * D], bhhn[:, 0:2 * D]), (gate_b[p + 1:p + 2, 7 * D:8 * D], bhhn[:, 2 * D:3 * D]),
                ]
            for dst, src in loads:
                pool.dma_start(dst, src).then_inc(weights_loaded, 16)
            assert len(loads) == WEIGHT_LOADS

            def stage(seen, q, row, lo, hi_, k=main):
                pool.wait_ge(k.used, seen * Q + q + 1)
                settle(pool)
                nc.gpsimd.tensor_copy(xs[:, q, :, lo:hi_],
                                      X[:, bass.ds(row * G + q * KK, KK), lo:hi_]).then_inc(k.staged, 1)

            def stage_h(seen, q, row, k=main):
                pool.wait_ge(k.signs_used, seen * Q + q + 1)
                settle(pool)
                nc.gpsimd.tensor_copy(hs[:, q, :, :], H[:, bass.ds(row * G + q * KK, KK), :]).then_inc(k.h_staged, 1)

            def row1(r):
                before = offs_before(r)

                def off(j):
                    pool.wait_ge(x_done, j + 1)
                    settle(pool)
                    for q in range(Q):
                        stage(before + j, q, j, 0, D)
                for_offs(pool, r, off)
            for_rows(pool, row1)

            def row(s, r):
                before = SEEN0[s] + all_before(r)
                here = row_of(s, r)
                a = LAYERS[s][0]

                def off(j):
                    pool.wait_ge(x_done, ROWS * (s - 1) + j + 1)
                    settle(pool)
                    for q in range(Q):
                        stage(before + j, q, row_of(s, j), 0, 2 * D)
                    if s == 4:
                        for q in range(Q):
                            stage_h(offs_before(r) + j, q, row_of(s, j))
                for_offs(pool, r, off)
                pool.wait_ge(x_done, ROWS * (s - 1))
                for q in range(Q):
                    stage(before + r, q, here, a * D, (a + 1) * D)

            for s in (2, 3, 4):
                for_rows(pool, lambda r: row(s, r))

            pool.wait_ge(x_done, ROWS * 4)

            def one(seen, signs_seen, row, k=main):
                for q in range(Q):
                    stage(seen, q, row, D, 2 * D, k)
                for q in range(Q):
                    stage_h(signs_seen, q, row, k)

            pool.wait_ge(flag_ready, 1)
            flag = pool.value_load(any_neg[0:1, 0:1], min_val=0, max_val=1)
            with pool.If(flag > 0):
                pool.wait_ge(used, SEEN0[5] * Q + Q)
                pool.wait_ge(signs_used, SIGN0[5] * Q + Q)
                with pool.Fori(0, ROWS) as m:
                    with pool.Fori(0, ROWS) as j:
                        one(m * ROWS + j, m * ROWS + j, (m + j) % ROWS, extra)
                pool.wait_ge(extra.used, ALL * Q + Q)
                pool.wait_ge(extra.signs_used, ALL * Q + Q)

            def row5(r):
                n = all_before(r)
                for_offs(pool, r, lambda j: one(SEEN0[5] + n + j, SIGN0[5] + n + j, j))
                one(SEEN0[5] + n + r, SIGN0[5] + n + r, r)
            for_rows(pool, row5)

        @block.tensor
        def _(pe):
            for free in (used, signs_used):
                pe.sem_inc(free, Q)

            pe.wait_ge(weights_loaded, 16 * WEIGHT_LOADS)
            pe.wait_ge(rhs_made, 2)
            for half in range(2):
                for c in range(2):
                    last = nc.tensor.matmul(turn[half * D:half * D + D, c:c + 1], wgt_sb[:, :],
                                            a_sb[:, (half + c) % 2:(half + c) % 2 + 1], start=True, stop=True)
            last.then_inc(score_made, 1)
            pe.wait_ge(score_copied, 1)

            def arrived(seen_loads, q):
                pe.wait_ge(loaded[q], (seen_loads + 1) * 16)

            def alone(c, q, into, first):
                for h in range(2):
                    for kk in range(KK):
                        last = nc.tensor.matmul(into[kk * D:kk * D + D, h * HALF:h * HALF + HALF],
                                                xs[:, q, kk, c * D:c * D + D],
                                                ring[:, q, kk, h * HALF:h * HALF + HALF],
                                                start=first and q == 0, stop=False, skip_group_check=True)
                return last

            def paired(q, first):
                for kk in range(KK):
                    for h in range(2):
                        last = nc.tensor.matmul(sums[:, h * HALF:h * HALF + HALF], xs[:, q, kk, :],
                                                ring[:, q, kk, h * HALF:h * HALF + HALF],
                                                start=first and q == 0 and kk == 0, stop=False, skip_group_check=True)
                return last

            def signs_times_h(signs_seen, first, k=main):
                for q in range(Q):
                    pe.wait_ge(k.masked, (signs_seen + 1) * Q + q + 1)
                    pe.wait_ge(k.h_staged, signs_seen * Q + q + 1)
                    for kk in range(KK):
                        for h in range(2):
                            cols = slice(h * HALF, h * HALF + HALF)
                            nc.tensor.matmul(sign_sums[:, cols], hs[:, q, kk, :], signs[:, q, kk, cols],
                                             start=first and q == 0 and kk == 0, stop=False, skip_group_check=True)
                    if q % 2:
                        for h in range(2):
                            cols = slice(h * HALF, h * HALF + HALF)
                            for c in range(2 * KK):
                                last = nc.tensor.matmul(counts[c * CQ:c * CQ + CQ, cols], ones_h[:, :],
                                                        signs[:, q - 1 + c // KK, c % KK, cols],
                                                        start=first and q == 1, stop=False, skip_group_check=True,
                                                        tile_position=(0, c * CQ))
                        last.then_inc(k.signs_used, 2)

            def turn_rows(pairs, into):
                for g in range(G):
                    for n, (src, rhs) in enumerate(pairs):
                        last = nc.tensor.matmul(into[:, g, 0:rhs.shape[1]], src[:, g * P:g * P + P], rhs,
                                                start=n == 0, stop=n == len(pairs) - 1)
                return last

            def turn_signs(src_counts):
                for g in range(G):
                    nc.tensor.matmul(sign_turned[:, g, 0:D], sign_sb[:, g * P:g * P + P], fold_h[:, :],
                                     start=True, stop=True)
                    last = nc.tensor.matmul(sign_turned[:, g, D:D + 1], src_counts[:, g * P:g * P + P], fold_count[:, :],
                                            start=True, stop=True)
                return last

            def row1(r):
                before = offs_before(r)

                def off(j):
                    for q in range(Q):
                        pe.wait_ge(staged, (before + j) * Q + q + 1)
                        arrived(r * (ROWS - 1) + ROWS + j, q)
                        last = alone(0, q, sums, isinstance(j, int))
                        last.then_inc(used, 1)
                    return last
                for_offs(pe, r, off)
                if not (isinstance(r, int) and r == 0):
                    pe.wait_ge(act_copied, r)
                    turn_rows([(sums_sb, fold[1])], turned).then_inc(t_ready, 1)
                    pe.wait_ge(t_free, 2 * r)
                pe.wait_ge(summed, (r + 1) * ROWS * Q + 4)
                for g in range(G):
                    for kk in range(KK):
                        last = nc.tensor.matmul(turn[:, g:g + 1], degree_acc[:, kk, g * P:g * P + P], ones[:, :],
                                                start=kk == 0, stop=kk == KK - 1)
                last.then_inc(t_ready, 1)
                pe.wait_ge(t_free, 2 * r + 1)
            for_rows(pe, row1)

            pe.wait_ge(neg_summed, 1)
            nc.tensor.matmul(turn[0:1, 0:1], neg_sum[:, :], ones[:, :], start=True, stop=True).then_inc(t_ready, 1)

            LOADS = ROWS * ROWS - PAIRS

            def row(s, r):
                before = SEEN0[s] + all_before(r)
                first_row = isinstance(r, int) and r == 0

                def off(j):
                    for q in range(Q):
                        pe.wait_ge(staged, (before + j) * Q + q + 1)
                        arrived(LOADS + before + j, q)
                        paired(q, isinstance(j, int)).then_inc(used, 1)
                    if s == 4:
                        if isinstance(j, int) and not (isinstance(r, int) and r == 1):
                            pe.wait_ge(s_free, r - 1)
                        signs_times_h(offs_before(r) + j, isinstance(j, int))
                for_offs(pe, r, off)
                pe.wait_ge(t_free, T0[s] + r)
                for q in range(Q):
                    pe.wait_ge(staged, (before + r) * Q + q + 1)
                    if s in DIAG0:
                        pe.wait_ge(diag_ready, DIAG0[s] + r * Q + q + 1)
                    else:
                        arrived(LOADS + before + r, q)
                    alone(LAYERS[s][0], q, turn, True).then_inc(used, 1)
                pairs = [(aux_sb, fold[s])]
                pe.wait_ge(dve_copied, DVE0[s] + r + 1)
                if not first_row:
                    pe.wait_ge(act_copied, ACT0[s] + r)
                    pairs = [(sums_sb, both[s][:, :])] + pairs
                turn_rows(pairs, turned).then_inc(t_ready, 1)
                if s == 4 and not first_row:
                    turn_signs(count_sb[4]).then_inc(s_ready, 1)

            for s in (2, 3, 4):
                for_rows(pe, lambda r: row(s, r))
            pe.wait_ge(s_free, SROW0[5])
            pe.wait_ge(t_free, T0[5])

            pe.wait_ge(flag_ready, 1)
            flag = pe.value_load(any_neg[0:1, 0:1], min_val=0, max_val=1)
            with pe.If(flag > 0):
                for free in (extra.used, extra.signs_used):
                    pe.sem_inc(free, Q)

                def negatives(n, first):
                    for q in range(Q):
                        pe.wait_ge(extra.staged, n * Q + q + 1)
                        pe.wait_ge(extra.masked, (n + 1) * Q + q + 1)
                        alone(1, q, sums, first).then_inc(extra.used, 1)
                    signs_times_h(n, first, extra)
                with pe.Fori(0, ROWS) as m:
                    negatives(m * ROWS, True)
                    with pe.Fori(1, ROWS) as j:
                        negatives(m * ROWS + j, False)
                    pe.wait_ge(extra.act_copied, m + 1)
                    pe.wait_ge(extra.dve_copied, m + 1)
                    turn_rows([(sums_sb, fold[5])], turned).then_inc(extra.t_ready, 1)
                    turn_signs(count_sb[5]).then_inc(extra.s_ready, 1)
                    pe.wait_ge(extra.t_free, m + 1)
                    pe.wait_ge(extra.s_free, m + 1)
            pe.nop()

            def transpose(src, g):
                return nc.tensor.matmul(turn[:, g * P:g * P + P], src[:, g, :], ident[:, :], start=True, stop=True)

            def cell_s(f):
                pe.wait_ge(s_built, f + 1)
                for g in range(G):
                    last = transpose(S, g)
                last.then_inc(st_made, 1)

            def cell_e(f):
                pe.wait_ge(st_copied, f + 1)
                for g in range(G):
                    last = nc.tensor.matmul(turn[:, g * 2:g * 2 + 2], ST[:, g, :], score_w[:, :], start=True, stop=True)
                last.then_inc(e_made, 1)

            def cell_h(f):
                pe.wait_ge(eh_built, f + 1)
                for g in range(G):
                    last = transpose(EH, g)
                last.then_inc(et_made, 1)
                pe.wait_ge(et_copied, f + 1)

            def cell_gates(f):
                for g in range(G):
                    bank = turn[:, g % 2 * HALF:g % 2 * HALF + HALF]
                    if g >= 2:
                        pe.wait_ge(gates_read, f * G + g - 1)
                    nc.tensor.matmul(bank, ET[:, g, :], w_rest[:, :], start=True, stop=False)
                    nc.tensor.matmul(bank, ones16[0:2 * CQ + 2, :], gate_b16[:, :], start=False, stop=False)
                    nc.tensor.matmul(bank[:, 0:4 * D], ST[:, g, :], w_edge[:, :], start=False, stop=True)\
                        .then_inc(gates_made, 1)
                pe.wait_ge(gates_read, f * G + G)

            def row5(r):
                n = all_before(r)
                one_row = isinstance(r, int) and r == 1

                def superblock(j, first, diagonal):
                    for q in range(Q):
                        pe.wait_ge(staged, (SEEN0[5] + n + j) * Q + q + 1)
                        if diagonal:
                            pe.wait_ge(diag_ready, DIAG0[5] + r * Q + q + 1)
                        else:
                            arrived(LOADS + SEEN0[5] + n + j, q)
                        alone(1, q, sums, first).then_inc(used, 1)
                    signs_times_h(SIGN0[5] + n + j, first)

                if isinstance(r, int) and r == 0:
                    superblock(0, True, True)
                else:
                    superblock(0, True, False)
                    if not one_row:
                        cell_gates(r - 2)
                    cell_s(r - 1)
                    if not one_row:
                        with pe.Fori(1, r) as j:
                            superblock(j, False, False)
                    cell_e(r - 1)
                    superblock(r, False, True)
                    cell_h(r - 1)
                pe.wait_ge(act_copied, ACT0[5] + r + 1)
                pe.wait_ge(dve_copied, DVE0[5] + r + 1)
                turn_rows([(sums_sb, fold[5])], turned).then_inc(t_ready, 1)
                turn_signs(count_sb[5]).then_inc(s_ready, 1)
                pe.wait_ge(t_free, T0[5] + r + 1)
                pe.wait_ge(s_free, SROW0[5] + r + 1)
            for_rows(pe, row5)
            cell_gates(ROWS - 2)
            cell_s(ROWS - 1)
            cell_e(ROWS - 1)
            cell_h(ROWS - 1)
            cell_gates(ROWS - 1)

        @block.scalar
        def _(act):
            def root(n):
                act.wait_ge(root_asked, n)
                nc.scalar.activation(root_out[:, :], root_in[:, :], ACT.Sqrt).then_inc(root_given, 1)

            act.sem_inc(scanned, Q)
            def row1(r):
                with act.Fori(0, ROWS) as k:
                    for q in range(Q):
                        n = (r * ROWS + k)
                        act.wait_ge(loaded[q], (n + 1) * 16)
                        nc.scalar.activation(unused, ring[:, q, :, :].rearrange("p k i -> p (k i)"), ACT.Relu, scale=-1.0,
                                             accum_out=neg_seen[:, bass.ds(n * Q + q, 1)]).then_inc(scanned, 1)
                        act.drain()
                if not (isinstance(r, int) and r == 0):
                    act.wait_ge(used, (offs_before(r) + r) * Q + Q)
                    nc.scalar.copy(sums_sb[:, :], sums[:, :]).then_inc(act_copied, 1)
                root(r + 1)
            for_rows(act, row1)

            def sign_block(n, count, q, wait_diag=None):
                act.wait_ge(signs_used, n * Q + q + 1)
                if wait_diag is None:
                    act.wait_ge(loaded[q], count)
                else:
                    act.wait_ge(diag_ready, wait_diag)
                nc.scalar.activation(signs[:, q, :, :], ring[:, q, :, :], ACT.Sign).then_inc(masked, 1)

            act.sem_inc(masked, Q)
            LOADS = ROWS * ROWS - PAIRS

            def row(s, r):
                def off(j):
                    for q in range(Q):
                        sign_block(offs_before(r) + j, (LOADS + SEEN0[4] + all_before(r) + j + 1) * 16, q)
                if s == 4:
                    for_offs(act, r, off)
                if not (isinstance(r, int) and r == 0):
                    act.wait_ge(used, (SEEN0[s] + all_before(r) + r) * Q + Q)
                    copied = nc.scalar.copy(sums_sb[:, :], sums[:, :])
                    if s != 4:
                        copied.then_inc(act_copied, 1)
                    else:
                        act.wait_ge(signs_used, (SIGN0[4] + offs_before(r) + r) * Q + Q)
                        nc.scalar.copy(sign_sb[:, :], sign_sums[:, :]).then_inc(act_copied, 1)
                if s < 4:
                    root(ROWS * (s - 1) + r + 1)
                else:
                    root(ROWS * 3 + 2 * r + 1)
                    root(ROWS * 3 + 2 * r + 2)

            for s in (2, 3, 4):
                for_rows(act, lambda r: row(s, r))

            def copy_sums(k, signs_total, n):
                act.wait_ge(k.signs_used, signs_total * Q + Q)
                nc.scalar.copy(sums_sb[:, :], sums[:, :])
                nc.scalar.copy(sign_sb[:, :], sign_sums[:, :]).then_inc(k.act_copied, 1)

            act.wait_ge(flag_ready, 1)
            flag = act.value_load(any_neg[0:1, 0:1], min_val=0, max_val=1)
            with act.If(flag > 0):
                with act.Fori(0, ROWS) as m:
                    copy_sums(extra, m * ROWS + ROWS, m)
                act.wait_ge(extra.s_ready, ROWS)
            act.nop()

            def gates_out(f):
                for g in range(G):
                    act.wait_ge(gates_made, f * G + g + 1)
                    bank = turn[:, g % 2 * HALF:g % 2 * HALF + HALF].rearrange("p (n c) -> p n c", n=2)
                    nc.scalar.activation(rz[:, g, :, :], bank[:, :, 0:2 * D], ACT.Tanh, scale=0.5)
                    nc.scalar.copy(cand[:, g, :, :], bank[:, :, 2 * D:4 * D]).then_inc(gates_read, 1)

            def s_out(f):
                act.wait_ge(st_made, f + 1)
                nc.scalar.copy(ST[:, :, :].rearrange("p g c -> p (g c)"), turn[:, :]).then_inc(st_copied, 1)

            def cand_tanh(f):
                act.wait_ge(cand_ready, f + 1)
                nc.scalar.activation(cand[:, :, :, 0:D], cand[:, :, :, 0:D], ACT.Tanh).then_inc(cand_made, 1)

            def exps(f):
                act.wait_ge(e_shifted, f + 1)
                nc.scalar.activation(ex[:, :, :], ee[:, 0:3, :], ACT.Exp).then_inc(exp_made, 1)

            def final_sqrt(f):
                act.wait_ge(var_ready, f + 1)
                nc.scalar.activation(final_root[:, :], final_in[:, :], ACT.Sqrt).then_inc(std_made, 1)

            def h_out(f):
                act.wait_ge(et_made, f + 1)
                nc.scalar.copy(ET[:, :, :].rearrange("p g c -> p (g c)"), turn[:, :]).then_inc(et_copied, 1)

            def row5(r):
                n = all_before(r)
                one_row = isinstance(r, int) and r == 1

                def off(j):
                    for q in range(Q):
                        sign_block(SIGN0[5] + n + j, (LOADS + SEEN0[5] + n + j + 1) * 16, q)
                first_row = isinstance(r, int) and r == 0
                if not first_row:
                    off(0)
                    if not one_row:
                        gates_out(r - 2)
                    s_out(r - 1)
                    if not one_row:
                        with act.Fori(1, r) as j:
                            off(j)
                        cand_tanh(r - 2)
                    exps(r - 1)
                for q in range(Q):
                    sign_block(SIGN0[5] + n + r, None, q, DIAG0[5] + r * Q + q + 1)
                if not first_row:
                    if not one_row:
                        final_sqrt(r - 2)
                    h_out(r - 1)
                copy_sums(main, SIGN0[5] + n + r + 1, r)
            for_rows(act, row5)
            gates_out(ROWS - 2)
            s_out(ROWS - 1)
            cand_tanh(ROWS - 2)
            exps(ROWS - 1)
            final_sqrt(ROWS - 2)
            h_out(ROWS - 1)
            gates_out(ROWS - 1)
            cand_tanh(ROWS - 1)
            final_sqrt(ROWS - 1)

        @block.vector
        def _(dve):
            V = nc.vector

            drained = [False]

            def wait(semaphore, n):
                if not drained[0]:
                    dve.drain()
                dve.wait_ge(semaphore, n)
                drained[0] = True

            def step(do, *operands):
                if not drained[0]:
                    dve.drain()
                drained[0] = False
                return do(*operands)

            def tt(o, a, b, op):
                return step(V.tensor_tensor, o, a, b, op)

            def ts(o, a, s1, s2, op0, op1=None):
                if s2 is None:
                    return step(V.tensor_scalar, o, a, s1, None, op0)
                return step(V.tensor_scalar, o, a, s1, s2, op0, op1)

            def total(o, a):
                return step(V.tensor_reduce, o, a, AX.X, ALU.add)

            def wide(s, width=D):
                return s.unsqueeze(2).to_broadcast([P, s.shape[1], width])

            def rsqrt(o, of, root_, spare):
                step(V.reciprocal, o, root_)
                tt(spare, o, o, ALU.mult)
                tt(spare, spare, of, ALU.mult)
                ts(spare, spare, -0.5, 1.5, ALU.mult, ALU.add)
                return tt(o, o, spare, ALU.mult)

            def layernorm(val, spare, o, n):
                total(stat[0][:, :], val)
                ts(stat[0][:, :], stat[0][:, :], 1.0 / D, None, ALU.mult)
                tt(val, val, wide(stat[0][:, :]), ALU.subtract)
                tt(spare, val, val, ALU.mult)
                total(stat[1][:, :], spare)
                ts(root_in[:, :], stat[1][:, :], 1.0 / D, LN_EPS, ALU.mult, ALU.add).then_inc(root_asked, 1)
                wait(root_given, n)
                rsqrt(stat[2][:, :], root_in[:, :], root_out[:, :], stat[3][:, :])
                return tt(o, val, wide(stat[2][:, :]), ALU.mult)

            dve.sem_inc(summed, Q)
            wait(weights_loaded, 16 * WEIGHT_LOADS)
            wait(rhs_made, 2)
            rest = gate_b_rest
            step(V.tensor_copy, gate_b16[0:2, :], gate_b[0:2, :])
            ts(rest[:, :], gate_b[:, :], 1.0, None, ALU.mult)
            parts16 = bias16
            step(V.tensor_copy, parts16, rest[:, :])
            tt(rest[:, :], rest[:, :], parts16, ALU.subtract)
            step(V.tensor_copy, parts16, rest[:, :])
            step(V.tensor_copy, gate_b16[CQ:CQ + 2, :], bias16[CQ:CQ + 2, :])
            tt(rest[:, :], rest[:, :], parts16, ALU.subtract)
            step(V.tensor_copy, gate_b16[2 * CQ:2 * CQ + 2, :], rest[2 * CQ:2 * CQ + 2, :])
            step(V.memset, part[:, 0:G, :], 0.0)
            step(V.memset, sign_part[:, (ROWS - 1) * G:TILES, :], 0.0)
            wait(score_made, 1)
            step(V.tensor_copy, score_w[:, :], turn[:, 0:2]).then_inc(score_copied, 1)
            wait(x_loaded, 16)

            def row1(r):
                def add(n, q, first):
                    wait(loaded[q], (n + 1) * 16)
                    if first:
                        step(V.tensor_copy, degree_acc[:, :, :], ring[:, q, :, :]).then_inc(summed, 1)
                    else:
                        tt(degree_acc[:, :, :], degree_acc[:, :, :], ring[:, q, :, :], ALU.add).then_inc(summed, 1)
                for q in range(Q):
                    add(r * ROWS, q, q == 0)
                with dve.Fori(1, ROWS) as k:
                    for q in range(Q):
                        add(r * ROWS + k, q, False)
                if not (isinstance(r, int) and r == 0):
                    wait(t_ready, 2 * r)
                    step(V.tensor_copy, part[:, tiles(r), :], turned[:, :, 0:D]).then_inc(t_free, 1)
                wait(t_ready, 2 * r + 1)
                step(V.tensor_scalar, stat[0][:, :], turn[:, 0:G], 1.0, None, ALU.add).then_inc(t_free, 1)
                ts(root_in[:, :], stat[0][:, :], 2e-35, None, ALU.max).then_inc(root_asked, 1)
                wait(root_given, r + 1)
                rsqrt(stat[1][:, :], root_in[:, :], root_out[:, :], stat[3][:, :])
                ts(stat[2][:, :], stat[0][:, :], 0.0, None, ALU.is_gt)
                tt(dinv[:, bass.ds(r * G, G)], stat[1][:, :], stat[2][:, :], ALU.mult)
                tt(X[:, tiles(r), 0:D], X[:, tiles(r), D:2 * D], wide(dinv[:, bass.ds(r * G, G)]),
                   ALU.mult).then_inc(x_done, 1)
            for_rows(dve, row1)

            wait(scanned, ROWS * ROWS * Q + Q)
            total(neg_sum[:, :], neg_seen[:, :]).then_inc(neg_summed, 1)
            wait(t_ready, 2 * ROWS)
            ts(any_neg[:, :], turn[0:1, 0:1], 0.0, None, ALU.is_gt).then_inc(flag_ready, 1)
            dve.drain().then_inc(t_free, 1)

            LOADS = ROWS * ROWS - PAIRS

            def fix_diag(s, r, tile0, count):
                for q in range(Q):
                    wait(loaded[q], count * 16)
                    for kk in range(KK):
                        t = q * KK + kk
                        sub = ring[:, q, kk, t * P:t * P + P]
                        if s == 2:
                            tt(z[:, 0:2, :].rearrange("p a b -> p (a b)"), sub, ident[:, :], ALU.mult)
                            total(diag[:, bass.ds(tile0 + t, 1)], z[:, 0:2, :].rearrange("p a b -> p (a b)"))
                        if s in (2, 4):
                            last = tt(sub, sub, ident[:, :], ALU.add)
                        else:
                            last = tt(sub, sub, off_diag[:, :], ALU.mult)
                    last.then_inc(diag_ready, 1)

            def row(s, r):
                first_row = isinstance(r, int) and r == 0
                here = row_of(s, r) if first_row else dve.snap(row_of(s, r))
                count = LOADS + SEEN0[s] + all_before(r) + r + 1
                if s in (2, 4):
                    fix_diag(s, r, here * G, count)
                wait(used, (SEEN0[s] + all_before(r) + r + 1) * Q + Q)
                if s == 4 and not first_row:
                    step(V.tensor_copy, aux_sb[:, :], turn[:, :])
                    step(V.tensor_copy, count_sb[4], counts[:, :]).then_inc(dve_copied, 1)
                else:
                    step(V.tensor_copy, aux_sb[:, :], turn[:, :]).then_inc(dve_copied, 1)
                wait(t_ready, T0[s] + r + 1)
                settle(dve)
                tt(v[:, :, :], turned[:, :, 0:D], part[:, tiles(here), :], ALU.add)
                if first_row:
                    step(V.memset, part[:, tiles(here), :], 0.0).then_inc(t_free, 1)
                else:
                    step(V.tensor_copy, part[:, tiles(here), :], turned[:, :, D:2 * D]).then_inc(t_free, 1)
                if s == 4 and not first_row:
                    wait(s_ready, r)
                    step(V.tensor_copy, sign_part[:, tiles(here), :], sign_turned[:, :, 0:D + 1]).then_inc(s_free, 1)
                if s == 2:
                    tt(v[:, :, :], v[:, :, :], wide(dinv[:, bass.ds(here * G, G)]), ALU.mult)
                    tt(v[:, :, :], v[:, :, :], X[:, tiles(here), D:2 * D], ALU.add)
                    layernorm(v[:, :, :], w[:, :, :], X[:, tiles(here), D:2 * D], ROWS + r + 1).then_inc(x_done, 1)
                if s == 3:
                    x1 = X[:, tiles(here), D:2 * D]
                    tt(w[:, :, :], v[:, :, :], x1, ALU.mult)
                    total(stat[0][:, :], w[:, :, :])
                    ts(stat[0][:, :], stat[0][:, :], 0.01, None, ALU.mult)
                    ts(v[:, :, :], x1, -0.1, 1.0, ALU.mult, ALU.add)
                    tt(v[:, :, :], v[:, :, :], wide(stat[0][:, :]), ALU.subtract)
                    tt(v[:, :, :], v[:, :, :], x1, ALU.add)
                    layernorm(v[:, :, :], w[:, :, :], X[:, tiles(here), 0:D], 2 * ROWS + r + 1).then_inc(x_done, 1)
                if s == 4:
                    tt(v[:, :, :], v[:, :, :], b2_sb[:, :].unsqueeze(1).to_broadcast([P, G, D]), ALU.add)
                    ts(v[:, :, :], v[:, :, :], 0.0, None, ALU.max)
                    tt(w[:, :, :], v[:, :, :], v[:, :, :], ALU.mult)
                    total(stat[0][:, :], w[:, :, :])
                    ts(root_in[:, :], stat[0][:, :], 1e-30, None, ALU.max).then_inc(root_asked, 1)
                    wait(root_given, 3 * ROWS + 2 * r + 1)
                    step(V.reciprocal, stat[1][:, :], root_out[:, :])
                    tt(stat[1][:, :], stat[1][:, :], root_in[:, :], ALU.mult)
                    tt(stat[1][:, :], stat[1][:, :], root_out[:, :], ALU.add)
                    ts(stat[1][:, :], stat[1][:, :], 0.5, NORM_EPS, ALU.mult, ALU.add)
                    step(V.reciprocal, stat[2][:, :], stat[1][:, :])
                    tt(v[:, :, :], v[:, :, :], wide(stat[2][:, :]), ALU.mult)
                    tt(v[:, :, :], v[:, :, :], X[:, tiles(here), 0:D], ALU.add)
                    x3 = X[:, tiles(here), D:2 * D]
                    layernorm(v[:, :, :], w[:, :, :], x3, 3 * ROWS + 2 * r + 2)
                    ts(w[:, :, :], x3, H_SCALE, None, ALU.mult)
                    step(V.tensor_copy, H[:, tiles(here), 0:D], w[:, :, :])
                    tt(z[:, :, :], w[:, :, :], H[:, tiles(here), 0:D], ALU.subtract)
                    ts(H[:, tiles(here), D:2 * D], z[:, :, :], L_SCALE, None, ALU.mult).then_inc(x_done, 1)

            for s in (2, 3, 4):
                for_rows(dve, lambda r: row(s, r))

            step(V.memset, X[:, :, 0:D], 0.0)
            dve.drain()
            flag = dve.value_load(any_neg[0:1, 0:1], min_val=0, max_val=1)
            with dve.If(flag > 0):
                dve.sem_inc(extra.masked, Q)

                def split(n, diagonal):
                    for q in range(Q):
                        wait(extra.loaded[q], (n + 1) * 16)
                        if diagonal:
                            for kk in range(KK):
                                t = q * KK + kk
                                sub = ring[:, q, kk, t * P:t * P + P]
                                tt(sub, sub, off_diag[:, :], ALU.mult)
                        wait(extra.signs_used, n * Q + q + 1)
                        ts(signs[:, q, :, :], ring[:, q, :, :], 0.0, None, ALU.is_lt)
                        ts(ring[:, q, :, :], ring[:, q, :, :], 0.0, None, ALU.min).then_inc(extra.masked, 1)
                with dve.Fori(0, ROWS) as m:
                    split(m * ROWS, True)
                    with dve.Fori(1, ROWS) as j:
                        split(m * ROWS + j, False)
                    wait(extra.signs_used, (m * ROWS + ROWS) * Q + Q)
                    step(V.tensor_copy, count_sb[5], counts[:, :]).then_inc(extra.dve_copied, 1)
                    wait(extra.t_ready, m + 1)
                    step(V.tensor_copy, X[:, tiles(m), 0:D], turned[:, :, 0:D]).then_inc(extra.t_free, 1)
                    wait(extra.s_ready, m + 1)
                    step(V.tensor_copy, neg_part[:, tiles(m), :], sign_turned[:, :, 0:D + 1]).then_inc(extra.s_free, 1)
            dve.drain()

            def counts_of(ap):
                return ap[:, :, D:D + 1].rearrange("p a b -> p (a b)")

            def end_row(r, signs_total):
                wait(signs_used, signs_total * Q + Q)
                step(V.tensor_copy, count_sb[5], counts[:, :]).then_inc(dve_copied, 1)
                neg, sgn = neg_part[:, tiles(r), :], sign_part[:, tiles(r), :]
                wait(t_ready, T0[5] + r + 1)
                tt(RP[:, :, :], turned[:, :, 0:D], part[:, tiles(r), :], ALU.add).then_inc(t_free, 1)
                wait(s_ready, SROW0[5] + r + 1)
                tt(sgn, sign_turned[:, :, 0:D + 1], sgn, ALU.add).then_inc(s_free, 1)
                tt(RP[:, :, :], RP[:, :, :], X[:, tiles(r), 0:D], ALU.subtract)
                tt(S[:, :, 0:D], sgn[:, :, 0:D], neg[:, :, 0:D], ALU.add)
                step(V.tensor_copy, S[:, :, D:2 * D], neg[:, :, 0:D]).then_inc(s_built, 1)
                tt(cnt[:, 0, :], counts_of(sgn), counts_of(neg), ALU.add)
                step(V.tensor_copy, cnt[:, 1, :], counts_of(neg))
                tt(cnt[:, 2, :], cnt[:, 0, :], cnt[:, 1, :], ALU.add)
                ts(cnt[:, 2, :], cnt[:, 2, :], -1.0, float(N), ALU.mult, ALU.add)

            def softmax(f):
                wait(e_made, f + 1)
                raw = turn[:, 0:2 * G].rearrange("p (g n) -> p n g", n=2)
                ts(fs[:, 0:2, :], raw, SLOPE, None, ALU.mult)
                tt(ee[:, 0:2, :], fs[:, 0:2, :], raw, ALU.max)
                ts(fs[:, 0:2, :], cnt[:, 0:2, :], 0.0, None, ALU.is_gt)
                tt(ee[:, 0:2, :], ee[:, 0:2, :], fs[:, 0:2, :], ALU.mult)
                ts(fs[:, 0:2, :], fs[:, 0:2, :], -NEG_INF, NEG_INF, ALU.mult, ALU.add)
                tt(ee[:, 0:2, :], ee[:, 0:2, :], fs[:, 0:2, :], ALU.add)
                step(V.memset, ee[:, 2, :], NEG_INF)
                tt(ee[:, 3, :], ee[:, 0, :], ee[:, 1, :], ALU.max)
                ts(ee[:, 3, :], ee[:, 3, :], NEG_INF, None, ALU.max)
                tt(ee[:, 0:3, :], ee[:, 0:3, :], ee[:, 3:4, :].to_broadcast([P, 3, G]),
                   ALU.subtract).then_inc(e_shifted, 1)
                step(V.tensor_copy, EH[:, :, D:2 * D], X[:, tiles(f), D:2 * D])
                wait(exp_made, f + 1)
                tt(fs[:, :, :], ex[:, :, :], cnt[:, :, :], ALU.mult)
                tt(fs[:, 0, :], fs[:, 0, :], fs[:, 1, :], ALU.add)
                tt(fs[:, 0, :], fs[:, 0, :], fs[:, 2, :], ALU.add)
                step(V.reciprocal, fs[:, 1, :], fs[:, 0, :])
                tt(ex[:, 0:2, :], ex[:, 0:2, :], fs[:, 1:2, :].to_broadcast([P, 2, G]), ALU.mult)
                tt(w[:, :, :], X[:, tiles(f), 0:D], wide(ex[:, 1, :]), ALU.mult)
                tt(RP[:, :, :], RP[:, :, :], wide(ex[:, 0, :]), ALU.mult)
                tt(EH[:, :, 0:D], w[:, :, :], RP[:, :, :], ALU.add).then_inc(eh_built, 1)

            def candidates(f):
                wait(gates_read, f * G + G)
                ts(rz[:, :, :, :], rz[:, :, :, :], 0.5, 0.5, ALU.mult, ALU.add)
                tt(cand[:, :, :, D:2 * D], rz[:, :, :, 0:D], cand[:, :, :, D:2 * D], ALU.mult)
                tt(cand[:, :, :, 0:D], cand[:, :, :, 0:D], cand[:, :, :, D:2 * D], ALU.add).then_inc(cand_ready, 1)

            def cells(f):
                h = X[:, tiles(f), D:2 * D]
                wait(cand_made, f + 1)
                for n in range(2):
                    tt(v[:, :, :], h, cand[:, :, n, 0:D], ALU.subtract)
                    tt(v[:, :, :], v[:, :, :], rz[:, :, n, D:2 * D], ALU.mult)
                    tt(cand[:, :, n, 0:D], cand[:, :, n, 0:D], v[:, :, :], ALU.add)
                tt(v[:, :, :], cand[:, :, 0, 0:D], cand[:, :, 1, 0:D], ALU.add)
                tt(v[:, :, :], v[:, :, :], wide(diag[:, bass.ds(f * G, G)]), ALU.mult)
                tt(v[:, :, :], v[:, :, :], h, ALU.add)
                total(stat[0][:, :], v[:, :, :])
                ts(stat[0][:, :], stat[0][:, :], 1.0 / D, None, ALU.mult)
                tt(v[:, :, :], v[:, :, :], wide(stat[0][:, :]), ALU.subtract)
                tt(w[:, :, :], v[:, :, :], v[:, :, :], ALU.mult)
                total(stat[1][:, :], w[:, :, :])
                ts(final_in[:, :], stat[1][:, :], 1.0 / D, LN_EPS, ALU.mult, ALU.add).then_inc(var_ready, 1)

            def last_norm(f):
                wait(std_made, f + 1)
                rsqrt(stat[2][:, :], final_in[:, :], final_root[:, :], stat[3][:, :])
                tt(X[:, tiles(f), 0:D], v[:, :, :], wide(stat[2][:, :]), ALU.mult).then_inc(y_ready, 1)

            def row5(r):
                n = all_before(r)
                more = not (isinstance(r, int) and r < 2)
                if more:
                    candidates(r - 2)
                fix_diag(5, r, None, LOADS + SEEN0[5] + n + r + 1)
                if more:
                    cells(r - 2)
                if not (isinstance(r, int) and r == 0):
                    softmax(r - 1)
                if more:
                    last_norm(r - 2)
                end_row(r, SIGN0[5] + n + r + 1)
            for_rows(dve, row5)
            candidates(ROWS - 2)
            cells(ROWS - 2)
            softmax(ROWS - 1)
            last_norm(ROWS - 2)
            candidates(ROWS - 1)
            cells(ROWS - 1)
            last_norm(ROWS - 1)


WEIGHT_LOADS = 38


def kernel(**inputs):
    import numpy as np
    import concourse.bacc as bacc
    from concourse.bass_utils import run_bass_kernel_spmd

    a = {k: np.asarray(val) for k, val in inputs.items()}
    adj = a["adj"].reshape(ROWS, SB, ROWS, Q, KK, P).transpose(0, 2, 3, 5, 4, 1)
    arrays = {
        "adj_t": np.ascontiguousarray(adj).reshape(ROWS * ROWS * Q, P, KK * SB),
        "x": np.ascontiguousarray(a["x"].reshape(TILES, P, D).transpose(1, 0, 2)).reshape(P, TILES * D),
        "w0": np.ascontiguousarray(a["L0_gnn_W"]),
        "w2t": np.ascontiguousarray(a["L2_gnn_W_weight"].T),
        "b2": np.ascontiguousarray(a["L2_gnn_W_bias"]),
        "wg": np.ascontiguousarray(a["L3_gnn_W_gat"]),
        "wgt": np.ascontiguousarray(a["L3_gnn_W_gat"].T),
        "a_gat": np.ascontiguousarray(a["L3_gnn_a_gat"]),
    }
    for c in "en":
        arrays[f"wih{c}"] = np.ascontiguousarray(a[f"L3_gnn_w_ih_{c}"].T)
        arrays[f"whh{c}"] = np.ascontiguousarray(a[f"L3_gnn_w_hh_{c}"].T)
        arrays[f"bih{c}"] = np.ascontiguousarray(a[f"L3_gnn_b_ih_{c}"]).reshape(1, 3 * D)
        arrays[f"bhh{c}"] = np.ascontiguousarray(a[f"L3_gnn_b_hh_{c}"]).reshape(1, 3 * D)
    order = ["adj_t", "x", "w0", "w2t", "b2", "wg", "wgt", "a_gat",
             "wihe", "whhe", "bihe", "bhhe", "wihn", "whhn", "bihn", "bhhn"]

    nc = bacc.Bacc("TRN2", target_bir_lowering=False, num_devices=1)
    args = [nc.dram_tensor(f"in_{n}", arrays[n].shape, mybir.dt.from_np(arrays[n].dtype), kind="ExternalInput").ap()
            for n in order]
    args.append(nc.dram_tensor("out_y", (P, TILES * D), F32, kind="ExternalOutput").ap())
    build(nc, *args)
    r = run_bass_kernel_spmd(nc, [{f"in_{n}": arrays[n] for n in order}], core_ids=[0])
    got = r.results[0]["out_y"]
    return np.ascontiguousarray(got.reshape(P, TILES, D).transpose(1, 0, 2)).reshape(N, D)
```

```python
from contextlib import ExitStack

import concourse.bass as bass
from concourse import mybir

F32 = mybir.dt.float32
BF16 = mybir.dt.bfloat16
F16 = mybir.dt.float16
I32 = mybir.dt.int32
ALU = mybir.AluOpType
ACT = mybir.ActivationFunctionType
AX = mybir.AxisListType

P = 128
N = 8192
D = 64
ROWS = 8
SB = N // ROWS
Q = 4
KK = SB // P // Q
G = SB // P
TILES = N // P
HALF = 512
H_SCALE = 4096.0
L_SCALE = 2048.0
CQ = 32
LN_EPS = 1e-5
NORM_EPS = 1e-7
NEG_INF = -9000000000000000.0
SLOPE = 0.2


class RingSems:
    pass


def build(nc, adj, x_in, w0, w2t, b2, wg, wgt, a_gat, wihe, whhe, bihe, bhhe, wihn, whhn, bihn, bhhn, out):
    ctx = ExitStack()
    with ctx:
        def sb(name, shape, dt=F32):
            return ctx.enter_context(nc.sbuf_tensor(name, shape, dt))

        def pb(name, shape):
            return ctx.enter_context(nc.psum_tensor(name, shape, F32))

        def sem(name):
            return ctx.enter_context(nc.semaphore(name))

        X = sb("X", [P, TILES, 2 * D])
        H = sb("H", [P, TILES, 2 * D], F16)
        part = sb("part", [P, TILES, D])
        sign_part = sb("sign_part", [P, TILES, D])
        sign_count = sb("sign_count", [P, TILES])
        neg_part = sb("neg_part", [P, TILES, D])
        neg_count = sb("neg_count", [P, TILES])
        dinv = sb("dinv", [P, TILES])
        diag = sb("diag", [P, TILES])
        ring = sb("ring", [P, Q, KK, SB])
        signs = sb("signs", [P, Q, KK, SB], F16)
        xs = sb("xs", [P, Q, KK, 2 * D])
        hs = sb("hs", [P, Q, KK, 2 * D], F16)
        sums_sb = sb("sums_sb", [P, SB])
        aux_sb = sb("aux_sb", [P, SB])
        sign_sb = sb("sign_sb", [P, SB])
        count_sb = aux_sb[:, 0:HALF]
        unused = signs[:, 0:1, :, :].rearrange("p q k i -> p (q k i)")
        v = sb("v", [P, G, D])
        w = sb("w", [P, G, D])
        z = sb("z", [P, G, D])
        stat = [sb(f"stat{n}", [P, G]) for n in range(4)]
        root_in = sb("root_in", [P, G])
        root_out = sb("root_out", [P, G])
        neg_sum = sb("neg_sum", [P, 1])
        any_neg = sb("any_neg", [1, 1], I32)
        ident = sb("ident", [P, P])
        off_diag = sb("off_diag", [P, P])
        ones = sb("ones", [P, CQ])
        both = {s: sb(f"both{s}", [P, P]) for s in (2, 3, 4)}
        fold_w0 = sb("fold_w0", [P, D])
        fold_id = sb("fold_id", [P, D])
        fold_h = sb("fold_h", [P, D])
        fold_count = sb("fold_count", [P, 2])
        fold_w2 = sb("fold_w2", [P, D])
        fold_wg = sb("fold_wg", [P, D])
        fold = {1: fold_w0[:, :], 2: fold_w0[:, :], 3: fold_id[:, :], 4: fold_w2[:, :], 5: fold_wg[:, :]}
        b2_sb = sb("b2_sb", [P, D])
        wgt_sb = sb("wgt_sb", [D, D])
        a_sb = sb("a_sb", [D, 2])
        score_w = sb("score_w", [P, 2])
        w_edge = sb("w_edge", [P, 4 * D])
        w_rest = sb("w_rest", [P, 8 * D])
        gate_b16 = sb("gate_b16", [2 * CQ + 2, 8 * D], BF16)
        ones16 = sb("ones16", [P, P], BF16)
        ones_h = sb("ones_h", [P, CQ], F16)

        sums = pb("sums", [P, SB])
        sign_sums = pb("sign_sums", [P, SB])
        counts = pb("counts", [P, SB])
        turn = pb("turn", [P, SB])
        turned = turn[:, :].rearrange("p (g c) -> p g c", g=G)
        sign_turned = counts[:, :].rearrange("p (g c) -> p g c", g=G)
        turned_deg = turned[:, 0, D:D + G]
        turned_cnt = turned[:, 1, D:D + G]

        def by_tile(ap):
            return ap.rearrange("p (t h) -> p h t", h=2)


        S = sb("S", [P, G, 2 * D])
        ST = sb("ST", [P, G, P])
        ET = sb("ET", [P, G, P])
        rz = sb("rz", [P, G, 2, 2 * D])
        EH = S
        cand = sb("cand", [P, G, 2, 2 * D])
        RP = z[:, :, :]
        early = S[:, :, :].rearrange("p g c -> p (g c)")
        gate_b = early[0:2 * CQ + 2, 0:8 * D]
        gate_b_rest = early[0:2 * CQ + 2, 8 * D:16 * D]
        bias16 = ST[0:2 * CQ + 2, 0:2, :].rearrange("p g c -> p (g c)").bitcast(BF16)
        neg_seen = ET[:, 0:2, :].rearrange("p g c -> p (g c)")
        cnt = sb("cnt", [P, 3, G])
        ee = sb("ee", [P, 4, G])
        ex = sb("ex", [P, 3, G])
        fs = sb("fs", [P, 3, G])
        final_in = sb("final_in", [P, G])
        final_root = sb("final_root", [P, G])

        def ring_sems(of):
            k = RingSems()
            k.loaded = [sem(f"{of}loaded{q}") for q in range(Q)]
            k.used = sem(f"{of}used")
            k.masked = sem(f"{of}masked")
            k.signs_used = sem(f"{of}signs_used")
            k.staged = sem(f"{of}staged")
            k.h_staged = sem(f"{of}h_staged")
            k.act_copied = sem(f"{of}act_copied")
            k.signs_copied = sem(f"{of}signs_copied")
            k.dve_copied = sem(f"{of}dve_copied")
            k.t_ready = sem(f"{of}t_ready")
            k.t_free = sem(f"{of}t_free")
            k.s_ready = sem(f"{of}s_ready")
            k.s_free = sem(f"{of}s_free")
            return k

        main = ring_sems("")
        extra = ring_sems("extra_")
        loaded, used, masked, signs_used = main.loaded, main.used, main.masked, main.signs_used
        staged, h_staged = main.staged, main.h_staged
        act_copied, dve_copied, t_ready, t_free, s_ready, s_free = (
            main.act_copied, main.dve_copied, main.t_ready, main.t_free, main.s_ready, main.s_free)
        half_made = sem("half_made")
        half_copied = sem("half_copied")
        x_loaded = sem("x_loaded")
        weights_loaded = sem("weights_loaded")
        zeroed = sem("zeroed")
        ident_made = sem("ident_made")
        rhs_made = sem("rhs_made")
        scanned = sem("scanned")
        diag_ready = sem("diag_ready")
        x_done = sem("x_done")
        root_asked = sem("root_asked")
        root_given = sem("root_given")
        neg_summed = sem("neg_summed")
        neg_total = sem("neg_total")
        flag_ready = sem("flag_ready")
        score_made = sem("score_made")
        s_built = sem("s_built")
        st_made = sem("st_made")
        st_copied = sem("st_copied")
        e_made = sem("e_made")
        e_shifted = sem("e_shifted")
        exp_made = sem("exp_made")
        eh_built = sem("eh_built")
        et_made = sem("et_made")
        et_copied = sem("et_copied")
        gates_made = sem("gates_made")
        gates_read = sem("gates_read")
        cand_ready = sem("cand_ready")
        cand_made = sem("cand_made")
        var_ready = sem("var_ready")
        std_made = sem("std_made")
        y_ready = sem("y_ready")
        stored = sem("stored")
        passed = {nc.gpsimd: sem("pool_passed"), nc.sync: sem("sp_passed"), nc.vector: sem("dve_passed")}

        PAIRS = ROWS * (ROWS - 1) // 2
        TRI = PAIRS + ROWS
        ALL = ROWS * ROWS
        SEEN0 = {2: ALL, 3: ALL + TRI, 4: ALL + 2 * TRI, 5: ALL + 3 * TRI}
        UNSTAGED = ALL - PAIRS
        T0 = {2: ROWS, 3: 2 * ROWS, 4: 3 * ROWS, 5: 4 * ROWS}
        ACT0 = {1: 0, 2: ROWS - 1, 3: 2 * (ROWS - 1), 4: 3 * (ROWS - 1), 5: 4 * (ROWS - 1)}
        DVE0 = {2: ROWS, 3: 2 * ROWS, 4: 3 * ROWS}
        DIAG0 = {2: 0, 4: Q * ROWS, 5: 2 * Q * ROWS}
        SCAN0 = {2: 0, 3: PAIRS}
        SIGN0 = {4: ALL, 5: ALL + PAIRS}
        SROW0 = {4: 0, 5: ROWS - 1}
        LAYERS = {2: (0, 1), 3: (1, 0), 4: (0, 1)}

        def offs_before(r):
            return r * (r - 1) // 2

        def all_before(r):
            return r * (r + 1) // 2

        def row_of(s, r):
            return (ROWS - 1) - r if s in (2, 4) else r

        def grid(row, col):
            return (row * ROWS + col) * Q

        def for_rows(e, body, alone=3, last_alone=False):
            for r in range(alone):
                body(r)
            with e.Fori(alone, ROWS - last_alone) as r:
                body(r)
            if last_alone:
                body(ROWS - 1)

        def for_offs(e, r, body):
            if isinstance(r, int) and r == 0:
                return
            body(0)
            if not (isinstance(r, int) and r == 1):
                with e.Fori(1, r) as j:
                    body(j)

        def for_sweep1(e, r, right, left):
            right(r * ROWS, r)
            if not (isinstance(r, int) and r == ROWS - 1):
                with e.Fori(r + 1, ROWS) as k:
                    right(r * (ROWS - 1) + k, k)
            for_offs(e, r, lambda j: left(left_at(r, j), j))

        def left_at(r, j):
            return r * (ROWS - 1) + ROWS + j

        def for_step(e, r, off, diagonal):
            if isinstance(r, int) and r == 0:
                diagonal(0)
            elif isinstance(r, int) and r == 1:
                diagonal(0)
                off(1, 0)
            else:
                off(0, 0)
                if not isinstance(r, int):
                    with e.Fori(1, r - 1) as j:
                        off(j, j)
                diagonal(r - 1)
                off(r, r - 1)

        def settle(e):
            e.sem_inc(passed[e], 1)

        def tiles(row):
            return bass.ds(row * G, G)

        block = ctx.enter_context(nc.Block())

        @block.sync
        def _(sp):
            sp.dma_start(X[:, :, D:2 * D], x_in.rearrange("p (t c) -> p t c", t=TILES)).then_inc(x_loaded, 16)

            def load(place, q, loaded=main.loaded):
                sp.dma_start(ring[:, q, :, :],
                             adj[bass.ds(place + q, 1)].rearrange("o p (k i) -> p (o k) i", k=KK)).then_inc(loaded[q], 16)

            def wait(semaphore, n):
                sp.wait_ge(semaphore, n)
                settle(sp)

            def row1(r):
                def one(n, k):
                    for q in range(Q):
                        wait(used, n * Q + q + 1)
                        wait(masked, n * Q + q + 1)
                        load(grid(r, k), q)
                for_sweep1(sp, r, one, one)
            for_rows(sp, row1, 2, last_alone=True)
            sp.wait_ge(masked, ALL * Q + Q)

            def row(s, r):
                before = SEEN0[s] + all_before(r)
                here = row_of(s, r)

                def one(n, act_seen, place):
                    for q in range(Q):
                        wait(used, (before + n) * Q + q + 1)
                        wait(scanned if s in (2, 3) else masked, act_seen * Q + q + 1)
                        load(place, q)

                def off(n, j):
                    seen = {2: offs_before(r) + j, 3: SCAN0[3] + all_before(r) + n,
                            4: SIGN0[4] + offs_before(r) + j, 5: SIGN0[5] + all_before(r) + n}[s]
                    one(n, seen, grid(here, row_of(s, j)))

                def diagonal(n):
                    offs = offs_before(r) + n
                    seen = {2: offs, 3: SCAN0[3] + all_before(r) + n,
                            4: SIGN0[4] + offs, 5: SIGN0[5] + all_before(r) + n}[s]
                    one(n, seen, grid(here, here))

                if s == 5:
                    for_offs(sp, r, lambda j: off(j, j))
                    diagonal(r)
                else:
                    for_step(sp, r, off, diagonal)

            for s in (2, 3, 4):
                for_rows(sp, lambda r: row(s, r))
                if s == 3:
                    sp.wait_ge(scanned, ALL * Q + Q)

            sp.wait_ge(flag_ready, 1)
            flag = sp.value_load(any_neg[0:1, 0:1], min_val=0, max_val=1)
            with sp.If(flag > 0):
                sp.wait_ge(used, SEEN0[5] * Q + Q)
                sp.wait_ge(masked, SIGN0[5] * Q + Q)
                with sp.Fori(0, ROWS) as m:
                    with sp.Fori(0, ROWS) as j:
                        for q in range(Q):
                            wait(extra.used, (m * ROWS + j) * Q + q + 1)
                            wait(extra.masked, (m * ROWS + j) * Q + q + 1)
                            load(grid(m, (m + j) % ROWS), q, extra.loaded)
                sp.wait_ge(extra.used, ALL * Q + Q)
                sp.wait_ge(extra.masked, ALL * Q + Q)

            for_rows(sp, lambda r: row(5, r), 2)
            with sp.Fori(0, ROWS) as f:
                wait(y_ready, f + 1)
                sp.dma_start(out.rearrange("p (t c) -> p t c", t=TILES)[:, tiles(f), :],
                             X[:, tiles(f), 0:D]).then_inc(stored, 16)
            sp.wait_ge(stored, 16 * ROWS)
        @block.gpsimd
        def _(pool):
            nc.gpsimd.memset(ident[:, :], 0.0)
            nc.gpsimd.memset(off_diag[:, :], 1.0)
            nc.gpsimd.memset(ones[:, :], 1.0)
            nc.gpsimd.memset(ones16[:, :], 1.0)
            nc.gpsimd.memset(ones_h[:, :], 1.0)
            for t in (both[2], both[3], both[4], fold_count, w_edge, w_rest, gate_b16):
                nc.gpsimd.memset(t[:, :], 0.0)
            nc.gpsimd.memset(gate_b, 0.0)
            nc.gpsimd.memset(neg_count[:, :], 0.0)
            nc.gpsimd.memset(neg_part[:, :, :], 0.0).then_inc(zeroed, 1)
            pool.wait_ge(zeroed, 1)
            nc.gpsimd.affine_select(out=ident[:, :], in_=ident[:, :], compare_op=ALU.not_equal, fill=1.0,
                                    base=0, pattern=[[-1, P]], channel_multiplier=1).then_inc(ident_made, 1)
            nc.gpsimd.affine_select(out=off_diag[:, :], in_=off_diag[:, :], compare_op=ALU.not_equal, fill=0.0,
                                    base=0, pattern=[[-1, P]], channel_multiplier=1).then_inc(ident_made, 1)
            pool.wait_ge(ident_made, 2)
            hi = ident[D:P, D:P]
            nc.gpsimd.tensor_copy(both[2][D:P, D:P], hi)
            nc.gpsimd.tensor_copy(both[3][D:P, 0:D], hi)
            nc.gpsimd.tensor_copy(fold_id[0:D, 0:D], ident[0:D, 0:D])
            nc.gpsimd.tensor_copy(fold_id[D:P, 0:D], hi)
            nc.gpsimd.tensor_scalar(fold_h[0:D, :], ident[0:D, 0:D], 1.0 / H_SCALE, None, ALU.mult)
            nc.gpsimd.tensor_scalar(fold_h[D:P, :], hi, 1.0 / (H_SCALE * L_SCALE), None, ALU.mult).then_inc(rhs_made, 1)
            pool.wait_ge(rhs_made, 1)
            for c in range(0, P, CQ):
                half = c // (2 * CQ)
                last = nc.gpsimd.memset(fold_count[c:c + 1, half:half + 1], 1.0)
            last.then_inc(rhs_made, 1)

            loads = [
                (both[2][0:D, 0:D], w0), (both[3][0:D, D:P], w2t), (both[4][0:D, 0:D], w2t), (both[4][D:P, D:P], wg),
                (fold_w0[0:D, :], w0), (fold_w0[D:P, :], w0), (fold_w2[0:D, :], w2t), (fold_w2[D:P, :], w2t),
                (fold_wg[0:D, :], wg), (fold_wg[D:P, :], wg), (wgt_sb[:, :], wgt),
                (b2_sb[:, :], b2.partition_broadcast(P)),
                (a_sb[:, 0:1], a_gat[0:D, :]), (a_sb[:, 1:2], a_gat[D:2 * D, :]),
                (w_edge[:, 0:3 * D], wihe),
                (w_rest[D:P, 0:2 * D], whhe[:, 0:2 * D]), (w_rest[D:P, 3 * D:4 * D], whhe[:, 2 * D:3 * D]),
                (w_rest[0:D, 4 * D:7 * D], wihn),
                (w_rest[D:P, 4 * D:6 * D], whhn[:, 0:2 * D]), (w_rest[D:P, 7 * D:8 * D], whhn[:, 2 * D:3 * D]),
            ]
            for p in (0, CQ, 2 * CQ):
                loads += [
                    (gate_b[p:p + 1, 0:3 * D], bihe), (gate_b[p:p + 1, 4 * D:7 * D], bihn),
                    (gate_b[p + 1:p + 2, 0:2 * D], bhhe[:, 0:2 * D]), (gate_b[p + 1:p + 2, 3 * D:4 * D], bhhe[:, 2 * D:3 * D]),
                    (gate_b[p + 1:p + 2, 4 * D:6 * D], bhhn[:, 0:2 * D]), (gate_b[p + 1:p + 2, 7 * D:8 * D], bhhn[:, 2 * D:3 * D]),
                ]
            for dst, src in loads:
                pool.dma_start(dst, src).then_inc(weights_loaded, 16)
            assert len(loads) == WEIGHT_LOADS

            def stage(seen, q, row, lo, hi_, k=main):
                pool.wait_ge(k.used, seen * Q + q + 1)
                settle(pool)
                nc.gpsimd.tensor_copy(xs[:, q, :, lo:hi_],
                                      X[:, bass.ds(row * G + q * KK, KK), lo:hi_]).then_inc(k.staged, 1)

            def stage_h(seen, q, row, k=main):
                pool.wait_ge(k.signs_used, seen * Q + q + 1)
                settle(pool)
                nc.gpsimd.tensor_copy(hs[:, q, :, :], H[:, bass.ds(row * G + q * KK, KK), :]).then_inc(k.h_staged, 1)

            def row1(r):
                def left(n, j):
                    pool.wait_ge(x_done, j + 1)
                    settle(pool)
                    for q in range(Q):
                        stage(n, q, j, 0, D)
                for_offs(pool, r, lambda j: left(left_at(r, j), j))
            for_rows(pool, row1, 2)

            def row(s, r):
                before = SEEN0[s] + all_before(r)
                here = row_of(s, r)
                a = LAYERS[s][0]

                def off(n, j):
                    pool.wait_ge(x_done, ROWS * (s - 1) + j + 1)
                    settle(pool)
                    for q in range(Q):
                        stage(before + n, q, row_of(s, j), 0, 2 * D)
                    if s == 4:
                        for q in range(Q):
                            stage_h(SIGN0[4] + offs_before(r) + j, q, row_of(s, j))

                def diagonal(n):
                    pool.wait_ge(x_done, ROWS * (s - 1))
                    for q in range(Q):
                        stage(before + n, q, here, a * D, (a + 1) * D)
                for_step(pool, r, off, diagonal)

            for s in (2, 3, 4):
                for_rows(pool, lambda r: row(s, r))

            pool.wait_ge(x_done, ROWS * 4)

            def one(seen, signs_seen, row, k=main):
                for q in range(Q):
                    stage(seen, q, row, D, 2 * D, k)
                for q in range(Q):
                    stage_h(signs_seen, q, row, k)

            pool.wait_ge(flag_ready, 1)
            flag = pool.value_load(any_neg[0:1, 0:1], min_val=0, max_val=1)
            with pool.If(flag > 0):
                pool.wait_ge(used, SEEN0[5] * Q + Q)
                pool.wait_ge(signs_used, SIGN0[5] * Q + Q)
                with pool.Fori(0, ROWS) as m:
                    with pool.Fori(0, ROWS) as j:
                        one(m * ROWS + j, m * ROWS + j, (m + j) % ROWS, extra)
                pool.wait_ge(extra.used, ALL * Q + Q)
                pool.wait_ge(extra.signs_used, ALL * Q + Q)

            def row5(r):
                n = all_before(r)
                for_offs(pool, r, lambda j: one(SEEN0[5] + n + j, SIGN0[5] + n + j, j))
                one(SEEN0[5] + n + r, SIGN0[5] + n + r, r)
            for_rows(pool, row5, 2)

        @block.tensor
        def _(pe):
            for free in (used, signs_used):
                pe.sem_inc(free, Q)
            pe.wait_ge(rhs_made, 2)

            def arrived(seen_loads, q):
                pe.wait_ge(loaded[q], (seen_loads + 1) * 16)

            def alone(c, q, into, first):
                for h in range(2):
                    for kk in range(KK):
                        last = nc.tensor.matmul(into[kk * D:kk * D + D, h * HALF:h * HALF + HALF],
                                                xs[:, q, kk, c * D:c * D + D],
                                                ring[:, q, kk, h * HALF:h * HALF + HALF],
                                                start=first and q == 0, stop=False, skip_group_check=True)
                return last

            def paired(q, first):
                for h in range(2):
                    for kk in range(KK):
                        last = nc.tensor.matmul(sums[:, h * HALF:h * HALF + HALF], xs[:, q, kk, :],
                                                ring[:, q, kk, h * HALF:h * HALF + HALF],
                                                start=first and q == 0 and kk == 0, stop=False, skip_group_check=True)
                    if h == 0:
                        last.then_inc(half_made, 1)
                return last

            def sum_over_k(into, one, block_, q, first):
                for half in range(2):
                    for kk in range(KK):
                        c = (2 * half + kk) * CQ
                        last = nc.tensor.matmul(into[c:c + CQ, :], one[:, :],
                                                block_[:, q, kk, half * HALF:half * HALF + HALF],
                                                start=first and q == 0, stop=False, skip_group_check=True,
                                                tile_position=(0, c))
                return last

            def turn_sums(into, src):
                for t in range(G // 2):
                    last = nc.tensor.matmul(into[:, 2 * t:2 * t + 2], src[:, t * P:t * P + P], fold_count[:, :],
                                            start=True, stop=True)
                return last

            def signs_times_h(signs_seen, first, k=main):
                h_seen = signs_seen if k is extra else signs_seen - SIGN0[4]
                for q in range(Q):
                    pe.wait_ge(k.masked, (signs_seen + 1) * Q + q + 1)
                    pe.wait_ge(k.h_staged, h_seen * Q + q + 1)
                    for kk in range(KK):
                        for h in range(2):
                            cols = slice(h * HALF, h * HALF + HALF)
                            last = nc.tensor.matmul(sign_sums[:, cols], hs[:, q, kk, :], signs[:, q, kk, cols],
                                                    start=first and q == 0 and kk == 0, stop=False, skip_group_check=True)
                    if k is extra:
                        last = sum_over_k(counts[:, 0:HALF], ones_h, signs, q, first)
                    last.then_inc(k.signs_used, 1)

            def turn_rows(pairs, into, node_tiles=range(G)):
                for g in node_tiles:
                    for n, (src, rhs) in enumerate(pairs):
                        last = nc.tensor.matmul(into[:, g, 0:rhs.shape[1]], src[:, g * P:g * P + P], rhs,
                                                start=n == 0, stop=n == len(pairs) - 1)
                return last

            def turn_signs():
                for g in range(G):
                    last = nc.tensor.matmul(sign_turned[:, g, 0:D], sign_sb[:, g * P:g * P + P], fold_h[:, :],
                                            start=True, stop=True)
                return last

            def score_weights():
                for half in range(2):
                    for c in range(2):
                        last = nc.tensor.matmul(counts[half * D:half * D + D, c:c + 1], wgt_sb[:, :],
                                                a_sb[:, (half + c) % 2:(half + c) % 2 + 1], start=True, stop=True)
                last.then_inc(score_made, 1)

            def row1(r):
                def one(n, first, layer=None, opens=False, end=None):
                    if end is not None:
                        wait_copied(end)
                    for q in range(Q):
                        arrived(n, q)
                        if layer is not None:
                            pe.wait_ge(staged, layer * Q + q + 1)
                            alone(0, q, sums, opens)
                        sum_over_k(sign_sums[:, 0:HALF], ones, ring, q, first).then_inc(used, 1)
                        pe.wait_ge(masked, (n + 1) * Q + q + 1)
                        sum_over_k(sign_sums[:, HALF:SB], ones_h, signs, q, first).then_inc(signs_used, 1)
                        if end is not None:
                            end_row1(end, q)

                def right(n, k):
                    opens_row = k is r
                    ends = opens_row and not (isinstance(r, int) and r == 0)
                    one(n, opens_row, end=r - 1 if ends else None)

                for_sweep1(pe, r, right, lambda n, j: one(n, False, offs_before(r) + j, isinstance(j, int)))
                if isinstance(r, int) and r == 0:
                    pe.wait_ge(weights_loaded, 16 * WEIGHT_LOADS)
                    score_weights()

            def end_row1(f, q=None):
                if q in (None, 0):
                    if not (isinstance(f, int) and f == 0):
                        turn_rows([(sums_sb, fold[1])], turned, range(0, G // 2))
                if q in (None, 1):
                    if not (isinstance(f, int) and f == 0):
                        turn_rows([(sums_sb, fold[1])], turned, range(G // 2, G))
                if q in (None, 2):
                    turn_sums(turned_deg, sign_sb[:, 0:HALF])
                    turn_sums(turned_cnt, sign_sb[:, HALF:SB]).then_inc(t_ready, 1)

            def wait_copied(f):
                if not (isinstance(f, int) and f == 0):
                    pe.wait_ge(act_copied, f)
                    pe.wait_ge(t_free, f)
                pe.wait_ge(dve_copied, f + 1)
            for_rows(pe, row1, 2, last_alone=True)
            wait_copied(ROWS - 1)
            end_row1(ROWS - 1)

            def row(s, r):
                before = SEEN0[s] + all_before(r)
                first_row = isinstance(r, int) and r == 0

                def off(n, j):
                    first = isinstance(j, int) and j == 0
                    for q in range(Q):
                        pe.wait_ge(staged, (before - UNSTAGED + n) * Q + q + 1)
                        arrived(before + n, q)
                        paired(q, first).then_inc(used, 1)
                    if s == 4:
                        if first and not (isinstance(r, int) and r == 1):
                            pe.wait_ge(s_free, r - 1)
                        signs_times_h(SIGN0[4] + offs_before(r) + j, first)

                def diagonal(n):
                    pe.wait_ge(t_free, T0[s] + r)
                    for q in range(Q):
                        pe.wait_ge(staged, (before - UNSTAGED + n) * Q + q + 1)
                        if s in DIAG0:
                            pe.wait_ge(diag_ready, DIAG0[s] + r * Q + q + 1)
                        else:
                            arrived(before + n, q)
                        alone(LAYERS[s][0], q, turn, True).then_inc(used, 1)
                for_step(pe, r, off, diagonal)
                pe.wait_ge(dve_copied, DVE0[s] + r + 1)
                if first_row:
                    turn_rows([(aux_sb, fold[s])], turned).then_inc(t_ready, 1)
                else:
                    pairs = [(sums_sb, both[s][:, :]), (aux_sb, fold[s])]
                    pe.wait_ge(act_copied, ACT0[s] + r)
                    turn_rows(pairs, turned, range(G // 2))
                    pe.wait_ge(half_copied, ACT0[s] - ACT0[2] + r)
                    turn_rows(pairs, turned, range(G // 2, G)).then_inc(t_ready, 1)
                if s == 4 and not first_row:
                    pe.wait_ge(main.signs_copied, r)
                    turn_signs().then_inc(s_ready, 1)
                if s == 4 and first_row:
                    pe.wait_ge(neg_summed, 1)
                    nc.tensor.matmul(counts[0:1, 0:1], neg_sum[:, :], ones[:, 0:1], start=True, stop=True)\
                        .then_inc(neg_total, 1)

            for s in (2, 3, 4):
                for_rows(pe, lambda r: row(s, r))
            pe.wait_ge(s_free, SROW0[5])
            pe.wait_ge(t_free, T0[5])

            pe.wait_ge(flag_ready, 1)
            flag = pe.value_load(any_neg[0:1, 0:1], min_val=0, max_val=1)
            with pe.If(flag > 0):
                for free in (extra.used, extra.signs_used):
                    pe.sem_inc(free, Q)

                def negatives(n, first):
                    for q in range(Q):
                        pe.wait_ge(extra.staged, n * Q + q + 1)
                        pe.wait_ge(extra.masked, (n + 1) * Q + q + 1)
                        alone(1, q, sums, first).then_inc(extra.used, 1)
                    signs_times_h(n, first, extra)
                with pe.Fori(0, ROWS) as m:
                    negatives(m * ROWS, True)
                    with pe.Fori(1, ROWS) as j:
                        negatives(m * ROWS + j, False)
                    pe.wait_ge(extra.act_copied, m + 1)
                    turn_rows([(sums_sb, fold[5])], turned).then_inc(extra.t_ready, 1)
                    pe.wait_ge(extra.signs_copied, m + 1)
                    pe.wait_ge(extra.dve_copied, m + 1)
                    turn_signs()
                    turn_sums(turned_cnt, count_sb).then_inc(extra.s_ready, 1)
                    pe.wait_ge(extra.t_free, m + 1)
                    pe.wait_ge(extra.s_free, m + 1)
            pe.nop()

            def transpose(src, g):
                return nc.tensor.transpose(turn[:, g * P:g * P + P], src[:, g, :], ident[:, :])

            def cell_s(f):
                pe.wait_ge(s_built, f + 1)
                for g in range(G):
                    last = transpose(S, g)
                last.then_inc(st_made, 1)

            def cell_e(f):
                pe.wait_ge(st_copied, f + 1)
                for g in range(G):
                    last = nc.tensor.matmul(turn[:, g * 2:g * 2 + 2], ST[:, g, :], score_w[:, :], start=True, stop=True)
                last.then_inc(e_made, 1)

            def cell_h(f):
                pe.wait_ge(eh_built, f + 1)
                for g in range(G):
                    last = transpose(EH, g)
                last.then_inc(et_made, 1)

            def cell_gates(f):
                pe.wait_ge(et_copied, f + 1)
                for g in range(G):
                    bank = turn[:, g % 2 * HALF:g % 2 * HALF + HALF]
                    if g >= 2:
                        pe.wait_ge(gates_read, f * G + g - 1)
                    nc.tensor.matmul(bank, ET[:, g, :], w_rest[:, :], start=True, stop=False)
                    nc.tensor.matmul(bank, ones16[0:2 * CQ + 2, :], gate_b16[:, :], start=False, stop=False)
                    nc.tensor.matmul(bank[:, 0:4 * D], ST[:, g, :], w_edge[:, :], start=False, stop=True)\
                        .then_inc(gates_made, 1)
                pe.wait_ge(gates_read, f * G + G)

            def row5(r):
                n = all_before(r)

                def products(j, first, diagonal):
                    for q in range(Q):
                        pe.wait_ge(staged, (SEEN0[5] - UNSTAGED + n + j) * Q + q + 1)
                        if diagonal:
                            pe.wait_ge(diag_ready, DIAG0[5] + r * Q + q + 1)
                        else:
                            arrived(SEEN0[5] + n + j, q)
                        alone(1, q, sums, first).then_inc(used, 1)

                if isinstance(r, int) and r == 0:
                    products(0, True, True)
                    signs_times_h(SIGN0[5] + n, True)
                else:
                    products(0, True, False)
                    cell_s(r - 1)
                    signs_times_h(SIGN0[5] + n, True)
                    cell_e(r - 1)
                    def both_products(j, diagonal=False):
                        products(j, False, diagonal)
                        signs_times_h(SIGN0[5] + n + j, False)

                    if isinstance(r, int):
                        for j in range(1, r):
                            both_products(j)
                        if r < 3:
                            both_products(r, True)
                            cell_h(r - 1)
                            cell_gates(r - 1)
                        else:
                            cell_h(r - 1)
                            products(r, False, True)
                            cell_gates(r - 1)
                            signs_times_h(SIGN0[5] + n + r, False)
                    else:
                        both_products(1)
                        both_products(2)
                        cell_h(r - 1)
                        products(3, False, False)
                        cell_gates(r - 1)
                        signs_times_h(SIGN0[5] + n + 3, False)
                        with pe.Fori(4, r) as j:
                            both_products(j)
                        both_products(r, True)
                pe.wait_ge(act_copied, ACT0[5] + r + 1)
                turn_rows([(sums_sb, fold[5])], turned).then_inc(t_ready, 1)
                pe.wait_ge(main.signs_copied, SROW0[5] + r + 1)
                turn_signs().then_inc(s_ready, 1)
            for_rows(pe, row5, 5)
            cell_s(ROWS - 1)
            cell_e(ROWS - 1)
            cell_h(ROWS - 1)
            cell_gates(ROWS - 1)

        @block.scalar
        def _(act):
            def root(n):
                act.wait_ge(root_asked, n)
                nc.scalar.activation(root_out[:, :], root_in[:, :], ACT.Sqrt).then_inc(root_given, 1)

            for done in (masked, scanned):
                act.sem_inc(done, Q)

            def sign_block(n, count, q, wait_diag=None):
                act.wait_ge(signs_used, n * Q + q + 1)
                if wait_diag is None:
                    act.wait_ge(loaded[q], count)
                else:
                    act.wait_ge(diag_ready, wait_diag)
                nc.scalar.activation(signs[:, q, :, :], ring[:, q, :, :], ACT.Sign).then_inc(masked, 1)

            def row1(r):
                def one(k):
                    for q in range(Q):
                        sign_block(r * ROWS + k, (r * ROWS + k + 1) * 16, q)
                one(0)
                if not (isinstance(r, int) and r == 0):
                    root(r)
                with act.Fori(1, ROWS) as k:
                    one(k)
                if not (isinstance(r, int) and r == 0):
                    act.wait_ge(used, (r + 1) * ROWS * Q + Q)
                    nc.scalar.copy(sums_sb[:, :], sums[:, :]).then_inc(act_copied, 1)
            for_rows(act, row1, 1)
            root(ROWS)
            act.wait_ge(signs_used, ALL * Q + Q)

            def scan(n, count, root_behind=None):
                for q in range(Q):
                    act.wait_ge(loaded[q], count * 16)
                    nc.scalar.activation(unused, ring[:, q, :, :].rearrange("p k i -> p (k i)"), ACT.Relu, scale=-1.0,
                                         accum_out=neg_seen[:, bass.ds(n * Q + q, 1)]).then_inc(scanned, 1)
                    act.drain()
                    if q == Q // 2 and root_behind is not None:
                        root(root_behind)

            def row(s, r):
                def off(n, j):
                    count = SEEN0[s] + all_before(r) + n + 1
                    late = None
                    if isinstance(j, int) and j == 0 and not (isinstance(r, int) and r < 2):
                        late = ROWS * (s - 1) + r
                    if s == 2:
                        scan(offs_before(r) + j, count, late)
                    elif s == 3:
                        scan(SCAN0[3] + all_before(r) + n, count, late)
                    else:
                        for q in range(Q):
                            sign_block(SIGN0[4] + offs_before(r) + j, count * 16, q)
                            if late is not None and q % 2:
                                root(ROWS * 3 + 2 * (r - 1) + 1 + q // 2)

                def diagonal(n):
                    if s == 3:
                        late = ROWS * (s - 1) + 1 if isinstance(r, int) and r == 1 else None
                        scan(SCAN0[3] + all_before(r) + n, SEEN0[s] + all_before(r) + n + 1, late)
                for_step(act, r, off, diagonal)
                if not (isinstance(r, int) and r == 0):
                    act.wait_ge(half_made, ((s - 2) * PAIRS + offs_before(r) + r) * Q)
                    nc.scalar.copy(sums_sb[:, 0:HALF], sums[:, 0:HALF]).then_inc(act_copied, 1)
                    if s == 4:
                        act.wait_ge(signs_used, (SIGN0[4] + offs_before(r) + r) * Q + Q)
                        nc.scalar.copy(sign_sb[:, :], sign_sums[:, :]).then_inc(main.signs_copied, 1)
                if isinstance(r, int) and r == 0:
                    if s == 2:
                        root(ROWS * (s - 1) + 1)
                    if s == 4:
                        root(ROWS * 3 + 1)
                        root(ROWS * 3 + 2)

            for s in (2, 3, 4):
                for_rows(act, lambda r: row(s, r))
                if s < 4:
                    root(ROWS * s)
            root(ROWS * 5 - 1)
            root(ROWS * 5)

            def copy_sums(k, blocks):
                act.wait_ge(k.used, blocks)
                nc.scalar.copy(sums_sb[:, :], sums[:, :]).then_inc(k.act_copied, 1)

            def copy_signs(k, blocks):
                act.wait_ge(k.signs_used, blocks)
                nc.scalar.copy(sign_sb[:, :], sign_sums[:, :]).then_inc(k.signs_copied, 1)

            act.wait_ge(flag_ready, 1)
            flag = act.value_load(any_neg[0:1, 0:1], min_val=0, max_val=1)
            with act.If(flag > 0):
                with act.Fori(0, ROWS) as m:
                    copy_sums(extra, (m * ROWS + ROWS) * Q + Q)
                    copy_signs(extra, (m * ROWS + ROWS) * Q + Q)
                act.wait_ge(extra.s_ready, ROWS)
            act.nop()

            def gates_out(f):
                for g in range(G):
                    act.wait_ge(gates_made, f * G + g + 1)
                    bank = turn[:, g % 2 * HALF:g % 2 * HALF + HALF].rearrange("p (n c) -> p n c", n=2)
                    nc.scalar.activation(rz[:, g, :, :], bank[:, :, 0:2 * D], ACT.Tanh, scale=0.5)
                    nc.scalar.copy(cand[:, g, :, :], bank[:, :, 2 * D:4 * D]).then_inc(gates_read, 1)

            def s_out(f):
                act.wait_ge(st_made, f + 1)
                nc.scalar.copy(ST[:, :, :].rearrange("p g c -> p (g c)"), turn[:, :]).then_inc(st_copied, 1)

            def cand_tanh(f):
                act.wait_ge(cand_ready, f + 1)
                nc.scalar.activation(cand[:, :, :, 0:D], cand[:, :, :, 0:D], ACT.Tanh).then_inc(cand_made, 1)

            def exps(f):
                act.wait_ge(e_shifted, f + 1)
                nc.scalar.activation(ex[:, :, :], ee[:, 0:3, :], ACT.Exp).then_inc(exp_made, 1)

            def final_sqrt(f):
                act.wait_ge(var_ready, f + 1)
                nc.scalar.activation(final_root[:, :], final_in[:, :], ACT.Sqrt).then_inc(std_made, 1)

            def h_out(f):
                act.wait_ge(et_made, f + 1)
                nc.scalar.copy(ET[:, :, :].rearrange("p g c -> p (g c)"), turn[:, :]).then_inc(et_copied, 1)

            def row5(r):
                n = all_before(r)

                def off(j, blocks=range(Q)):
                    for q in blocks:
                        sign_block(SIGN0[5] + n + j, (SEEN0[5] + n + j + 1) * 16, q)

                def diagonal():
                    for q in range(Q):
                        sign_block(SIGN0[5] + n + r, None, q, DIAG0[5] + r * Q + q + 1)
                    copy_sums(main, (SEEN0[5] + n + r + 1) * Q + Q)

                if isinstance(r, int) and r == 0:
                    diagonal()
                elif isinstance(r, int) and r < 3:
                    off(0)
                    s_out(r - 1)
                    if r == 2:
                        final_sqrt(r - 2)
                        off(1)
                    diagonal()
                    exps(r - 1)
                    h_out(r - 1)
                    gates_out(r - 1)
                else:
                    off(0)
                    s_out(r - 1)
                    final_sqrt(r - 2)
                    off(1)
                    off(2, range(Q // 2))
                    exps(r - 1)
                    off(2, range(Q // 2, Q))
                    if isinstance(r, int):
                        for j in range(3, r):
                            off(j)
                        h_out(r - 1)
                        diagonal()
                        gates_out(r - 1)
                    else:
                        h_out(r - 1)
                        off(3)
                        gates_out(r - 1)
                        cand_tanh(r - 1)
                        with act.Fori(4, r) as j:
                            off(j)
                        diagonal()
                if isinstance(r, int) and r > 0:
                    cand_tanh(r - 1)
                copy_signs(main, (SIGN0[5] + n + r + 1) * Q + Q)
            for_rows(act, row5, 5)
            s_out(ROWS - 1)
            final_sqrt(ROWS - 2)
            exps(ROWS - 1)
            h_out(ROWS - 1)
            gates_out(ROWS - 1)
            cand_tanh(ROWS - 1)
            final_sqrt(ROWS - 1)

        @block.vector
        def _(dve):
            V = nc.vector

            drained = [False]

            def wait(semaphore, n):
                if not drained[0]:
                    dve.drain()
                dve.wait_ge(semaphore, n)
                drained[0] = True

            def step(do, *operands):
                if not drained[0]:
                    dve.drain()
                drained[0] = False
                return do(*operands)

            def tt(o, a, b, op):
                return step(V.tensor_tensor, o, a, b, op)

            def ts(o, a, s1, s2, op0, op1=None):
                if s2 is None:
                    return step(V.tensor_scalar, o, a, s1, None, op0)
                return step(V.tensor_scalar, o, a, s1, s2, op0, op1)

            def stt(o, a, s1, b, op0, op1):
                return step(V.scalar_tensor_tensor, o, a, s1, b, op0, op1)

            def total(o, a):
                return step(V.tensor_reduce, o, a, AX.X, ALU.add)

            def wide(s, width=D):
                return s.unsqueeze(2).to_broadcast([P, s.shape[1], width])

            def rsqrt(o, of, root_, spare):
                step(V.reciprocal, o, root_)
                stt(spare, of, -0.5, o, ALU.mult, ALU.mult)
                tt(spare, spare, o, ALU.mult)
                return stt(o, spare, 1.5, o, ALU.add, ALU.mult)

            def layernorm(val, spare, o, n):
                total(stat[0][:, :], val)
                stt(val, wide(stat[0][:, :]), -1.0 / D, val, ALU.mult, ALU.add)
                tt(spare, val, val, ALU.mult)
                total(stat[1][:, :], spare)
                ts(root_in[:, :], stat[1][:, :], 1.0 / D, LN_EPS, ALU.mult, ALU.add).then_inc(root_asked, 1)
                wait(root_given, n)
                rsqrt(stat[2][:, :], root_in[:, :], root_out[:, :], stat[3][:, :])
                return tt(o, val, wide(stat[2][:, :]), ALU.mult)

            step(V.memset, part[:, 0:G, :], 0.0)
            step(V.memset, sign_part[:, (ROWS - 1) * G:TILES, :], 0.0)

            def biases():
                wait(weights_loaded, 16 * WEIGHT_LOADS)
                rest = gate_b_rest
                step(V.tensor_copy, gate_b16[0:2, :], gate_b[0:2, :])
                ts(rest[:, :], gate_b[:, :], 1.0, None, ALU.mult)
                parts16 = bias16
                step(V.tensor_copy, parts16, rest[:, :])
                tt(rest[:, :], rest[:, :], parts16, ALU.subtract)
                step(V.tensor_copy, parts16, rest[:, :])
                step(V.tensor_copy, gate_b16[CQ:CQ + 2, :], bias16[CQ:CQ + 2, :])
                tt(rest[:, :], rest[:, :], parts16, ALU.subtract)
                step(V.tensor_copy, gate_b16[2 * CQ:2 * CQ + 2, :], rest[2 * CQ:2 * CQ + 2, :])

            wait(rhs_made, 2)
            wait(x_loaded, 16)

            def row1(r):
                wait(signs_used, (r + 1) * ROWS * Q + Q)
                step(V.tensor_copy, sign_sb[:, :], sign_sums[:, :]).then_inc(dve_copied, 1)
                wait(t_ready, r + 1)
                settle(dve)
                if not (isinstance(r, int) and r == 0):
                    step(V.tensor_copy, part[:, tiles(r), :], turned[:, :, 0:D])
                step(V.tensor_copy, sign_count[:, tiles(r)].rearrange("p (h t) -> p h t", h=2), by_tile(turned_cnt))
                step(V.tensor_scalar, stat[0][:, :].rearrange("p (h t) -> p h t", h=2), by_tile(turned_deg), 1.0, None,
                     ALU.add).then_inc(t_free, 1)
                ts(root_in[:, :], stat[0][:, :], 2e-35, None, ALU.max).then_inc(root_asked, 1)
                wait(root_given, r + 1)
                rsqrt(stat[1][:, :], root_in[:, :], root_out[:, :], stat[3][:, :])
                ts(stat[2][:, :], stat[0][:, :], 0.0, None, ALU.is_gt)
                tt(dinv[:, bass.ds(r * G, G)], stat[1][:, :], stat[2][:, :], ALU.mult)
                tt(X[:, tiles(r), 0:D], X[:, tiles(r), D:2 * D], wide(dinv[:, bass.ds(r * G, G)]),
                   ALU.mult).then_inc(x_done, 1)
                if isinstance(r, int) and r == 0:
                    biases()
                    wait(score_made, 1)
                    step(V.tensor_copy, score_w[:, :], counts[:, 0:2])
            for_rows(dve, row1, 1)

            def fix_diag(s, tile0, count, blocks=range(Q)):
                for q in blocks:
                    wait(loaded[q], count * 16)
                    subs = [ring[:, q, kk, (q * KK + kk) * P:(q * KK + kk) * P + P] for kk in range(KK)]
                    own = z[:, 0:2 * KK, :].rearrange("p (k a) b -> p k (a b)", k=KK)
                    if s == 2:
                        for kk in range(KK):
                            tt(own[:, kk, :], subs[kk], ident[:, :], ALU.mult)
                    for sub in subs:
                        if s in (2, 4):
                            last = tt(sub, sub, ident[:, :], ALU.add)
                        else:
                            last = tt(sub, sub, off_diag[:, :], ALU.mult)
                    last.then_inc(diag_ready, 1)
                    if s == 2:
                        total(diag[:, bass.ds(tile0 + q * KK, KK)], own)

            def row(s, r):
                first_row = isinstance(r, int) and r == 0
                here = row_of(s, r) if first_row else dve.snap(row_of(s, r))
                diag_at = SEEN0[s] + all_before(r) + (1 if first_row else r)
                if s in (2, 4) and not (isinstance(r, int) and r == 1):
                    fix_diag(s, here * G, diag_at)
                if s == 4 and first_row:
                    wait(scanned, ALL * Q + Q)
                    total(neg_sum[:, :], neg_seen[:, :]).then_inc(neg_summed, 1)
                wait(used, diag_at * Q + Q)
                step(V.tensor_copy, aux_sb[:, :], turn[:, :]).then_inc(dve_copied, 1)
                if not first_row:
                    wait(used, (SEEN0[s] + all_before(r) + r + 1) * Q + Q)
                    step(V.tensor_copy, sums_sb[:, HALF:SB], sums[:, HALF:SB]).then_inc(half_copied, 1)
                wait(t_ready, T0[s] + r + 1)
                settle(dve)
                summed = tt(v[:, :, :], turned[:, :, 0:D], part[:, tiles(here), :], ALU.add)
                if first_row:
                    summed.then_inc(t_free, 1)
                    if s in (2, 4):
                        fix_diag(s, row_of(s, 1) * G, diag_at + 1)
                else:
                    step(V.tensor_copy, part[:, tiles(here), :], turned[:, :, D:2 * D]).then_inc(t_free, 1)
                if s == 4 and not first_row:
                    wait(s_ready, r)
                    step(V.tensor_copy, sign_part[:, tiles(here), :], sign_turned[:, :, 0:D]).then_inc(s_free, 1)
                if s == 2:
                    tt(v[:, :, :], v[:, :, :], wide(dinv[:, bass.ds(here * G, G)]), ALU.mult)
                    tt(v[:, :, :], v[:, :, :], X[:, tiles(here), D:2 * D], ALU.add)
                    layernorm(v[:, :, :], w[:, :, :], X[:, tiles(here), D:2 * D], ROWS + r + 1).then_inc(x_done, 1)
                if s == 3:
                    x1 = X[:, tiles(here), D:2 * D]
                    tt(w[:, :, :], v[:, :, :], x1, ALU.mult)
                    total(stat[0][:, :], w[:, :, :])
                    ts(v[:, :, :], x1, -0.1, 1.0, ALU.mult, ALU.add)
                    stt(v[:, :, :], wide(stat[0][:, :]), -0.01, v[:, :, :], ALU.mult, ALU.add)
                    tt(v[:, :, :], v[:, :, :], x1, ALU.add)
                    layernorm(v[:, :, :], w[:, :, :], X[:, tiles(here), 0:D], 2 * ROWS + r + 1).then_inc(x_done, 1)
                if s == 4:
                    tt(v[:, :, :], v[:, :, :], b2_sb[:, :].unsqueeze(1).to_broadcast([P, G, D]), ALU.add)
                    stt(w[:, :, :], v[:, :, :], 0.0, v[:, :, :], ALU.max, ALU.mult)
                    total(stat[0][:, :], w[:, :, :])
                    ts(root_in[:, :], stat[0][:, :], 1e-30, None, ALU.max).then_inc(root_asked, 1)
                    wait(root_given, 3 * ROWS + 2 * r + 1)
                    step(V.reciprocal, stat[1][:, :], root_out[:, :])
                    tt(stat[1][:, :], stat[1][:, :], root_in[:, :], ALU.mult)
                    tt(stat[1][:, :], stat[1][:, :], root_out[:, :], ALU.add)
                    ts(stat[1][:, :], stat[1][:, :], 0.5, NORM_EPS, ALU.mult, ALU.add)
                    step(V.reciprocal, stat[2][:, :], stat[1][:, :])
                    stt(v[:, :, :], v[:, :, :], 0.0, wide(stat[2][:, :]), ALU.max, ALU.mult)
                    tt(v[:, :, :], v[:, :, :], X[:, tiles(here), 0:D], ALU.add)
                    x3 = X[:, tiles(here), D:2 * D]
                    layernorm(v[:, :, :], w[:, :, :], x3, 3 * ROWS + 2 * r + 2)
                    ts(H[:, tiles(here), 0:D], x3, H_SCALE, None, ALU.mult)
                    stt(z[:, :, :], x3, H_SCALE, H[:, tiles(here), 0:D], ALU.mult, ALU.subtract)
                    ts(H[:, tiles(here), D:2 * D], z[:, :, :], L_SCALE, None, ALU.mult).then_inc(x_done, 1)
                if first_row:
                    step(V.memset, part[:, tiles(here), :], 0.0)
                if s == 4 and first_row:
                    wait(neg_total, 1)
                    ts(any_neg[:, :], counts[0:1, 0:1], 0.0, None, ALU.is_gt)
                    dve.drain().then_inc(flag_ready, 1)

            for s in (2, 3, 4):
                for_rows(dve, lambda r: row(s, r))
                if s == 2:
                    ts(dinv[:, :], diag[:, :], 0.0, None, ALU.is_gt)
                    tt(sign_count[:, :], sign_count[:, :], dinv[:, :], ALU.subtract)
                    ts(dinv[:, :], diag[:, :], 0.0, None, ALU.is_lt)
                    tt(sign_count[:, :], sign_count[:, :], dinv[:, :], ALU.add)

            dve.drain()
            flag = dve.value_load(any_neg[0:1, 0:1], min_val=0, max_val=1)
            with dve.If(flag > 0):
                dve.sem_inc(extra.masked, Q)

                def split(n, diagonal):
                    for q in range(Q):
                        wait(extra.loaded[q], (n + 1) * 16)
                        if diagonal:
                            for kk in range(KK):
                                t = q * KK + kk
                                sub = ring[:, q, kk, t * P:t * P + P]
                                tt(sub, sub, off_diag[:, :], ALU.mult)
                        wait(extra.signs_used, n * Q + q + 1)
                        ts(signs[:, q, :, :], ring[:, q, :, :], 0.0, None, ALU.is_lt)
                        ts(ring[:, q, :, :], ring[:, q, :, :], 0.0, None, ALU.min).then_inc(extra.masked, 1)
                with dve.Fori(0, ROWS) as m:
                    split(m * ROWS, True)
                    with dve.Fori(1, ROWS) as j:
                        split(m * ROWS + j, False)
                    wait(extra.signs_used, (m * ROWS + ROWS) * Q + Q)
                    step(V.tensor_copy, count_sb, counts[:, 0:HALF]).then_inc(extra.dve_copied, 1)
                    wait(extra.t_ready, m + 1)
                    wait(extra.s_ready, m + 1)
                    step(V.tensor_copy, X[:, tiles(m), 0:D], turned[:, :, 0:D]).then_inc(extra.t_free, 1)
                    step(V.tensor_copy, neg_part[:, tiles(m), :], sign_turned[:, :, 0:D])
                    step(V.tensor_copy, neg_count[:, tiles(m)].rearrange("p (h t) -> p h t", h=2),
                         by_tile(turned_cnt)).then_inc(extra.s_free, 1)
            dve.drain()

            def end_row(r):
                neg, sgn = neg_part[:, tiles(r), :], sign_part[:, tiles(r), :]
                wait(t_ready, T0[5] + r + 1)
                tt(RP[:, :, :], turned[:, :, 0:D], part[:, tiles(r), :], ALU.add).then_inc(t_free, 1)
                wait(s_ready, SROW0[5] + r + 1)
                tt(sgn, sign_turned[:, :, 0:D], sgn, ALU.add).then_inc(s_free, 1)
                tt(RP[:, :, :], RP[:, :, :], X[:, tiles(r), 0:D], ALU.subtract)
                tt(S[:, :, 0:D], sgn[:, :, 0:D], neg[:, :, 0:D], ALU.add)
                step(V.tensor_copy, S[:, :, D:2 * D], neg[:, :, 0:D]).then_inc(s_built, 1)
                tt(cnt[:, 0, :], sign_count[:, tiles(r)], neg_count[:, tiles(r)], ALU.add)
                step(V.tensor_copy, cnt[:, 1, :], neg_count[:, tiles(r)])
                tt(cnt[:, 2, :], cnt[:, 0, :], cnt[:, 1, :], ALU.add)
                ts(cnt[:, 2, :], cnt[:, 2, :], -1.0, float(N), ALU.mult, ALU.add)

            def softmax(f):
                wait(e_made, f + 1)
                raw = turn[:, 0:2 * G].rearrange("p (g n) -> p n g", n=2)
                ts(fs[:, 0:2, :], raw, SLOPE, None, ALU.mult)
                tt(ee[:, 0:2, :], fs[:, 0:2, :], raw, ALU.max)
                ts(fs[:, 0:2, :], cnt[:, 0:2, :], 0.0, None, ALU.is_gt)
                tt(ee[:, 0:2, :], ee[:, 0:2, :], fs[:, 0:2, :], ALU.mult)
                ts(fs[:, 0:2, :], fs[:, 0:2, :], -NEG_INF, NEG_INF, ALU.mult, ALU.add)
                tt(ee[:, 0:2, :], ee[:, 0:2, :], fs[:, 0:2, :], ALU.add)
                step(V.memset, ee[:, 2, :], NEG_INF)
                tt(ee[:, 3, :], ee[:, 0, :], ee[:, 1, :], ALU.max)
                ts(ee[:, 3, :], ee[:, 3, :], NEG_INF, None, ALU.max)
                tt(ee[:, 0:3, :], ee[:, 0:3, :], ee[:, 3:4, :].to_broadcast([P, 3, G]),
                   ALU.subtract).then_inc(e_shifted, 1)
                step(V.tensor_copy, EH[:, :, D:2 * D], X[:, tiles(f), D:2 * D])
                wait(exp_made, f + 1)
                tt(fs[:, :, :], ex[:, :, :], cnt[:, :, :], ALU.mult)
                tt(fs[:, 0, :], fs[:, 0, :], fs[:, 1, :], ALU.add)
                tt(fs[:, 0, :], fs[:, 0, :], fs[:, 2, :], ALU.add)
                step(V.reciprocal, fs[:, 1, :], fs[:, 0, :])
                tt(ex[:, 0:2, :], ex[:, 0:2, :], fs[:, 1:2, :].to_broadcast([P, 2, G]), ALU.mult)
                tt(w[:, :, :], X[:, tiles(f), 0:D], wide(ex[:, 1, :]), ALU.mult)
                tt(RP[:, :, :], RP[:, :, :], wide(ex[:, 0, :]), ALU.mult)
                tt(EH[:, :, 0:D], w[:, :, :], RP[:, :, :], ALU.add).then_inc(eh_built, 1)

            def candidates(f):
                wait(gates_read, f * G + G)
                stt(cand[:, :, :, D:2 * D], rz[:, :, :, 0:D], 1.0, cand[:, :, :, D:2 * D], ALU.add, ALU.mult)
                stt(cand[:, :, :, 0:D], cand[:, :, :, D:2 * D], 0.5, cand[:, :, :, 0:D],
                    ALU.mult, ALU.add).then_inc(cand_ready, 1)

            def cells(f):
                h = X[:, tiles(f), D:2 * D]
                wait(cand_made, f + 1)
                for n in range(2):
                    tt(v[:, :, :], h, cand[:, :, n, 0:D], ALU.subtract)
                    stt(v[:, :, :], rz[:, :, n, D:2 * D], 1.0, v[:, :, :], ALU.add, ALU.mult)
                    stt(cand[:, :, n, 0:D], v[:, :, :], 0.5, cand[:, :, n, 0:D], ALU.mult, ALU.add)
                tt(v[:, :, :], cand[:, :, 0, 0:D], cand[:, :, 1, 0:D], ALU.add)
                tt(v[:, :, :], v[:, :, :], wide(diag[:, bass.ds(f * G, G)]), ALU.mult)
                tt(v[:, :, :], v[:, :, :], h, ALU.add)
                total(stat[0][:, :], v[:, :, :])
                stt(v[:, :, :], wide(stat[0][:, :]), -1.0 / D, v[:, :, :], ALU.mult, ALU.add)
                tt(w[:, :, :], v[:, :, :], v[:, :, :], ALU.mult)
                total(stat[1][:, :], w[:, :, :])
                ts(final_in[:, :], stat[1][:, :], 1.0 / D, LN_EPS, ALU.mult, ALU.add).then_inc(var_ready, 1)

            def last_norm(f):
                wait(std_made, f + 1)
                rsqrt(stat[2][:, :], final_in[:, :], final_root[:, :], stat[3][:, :])
                tt(X[:, tiles(f), 0:D], v[:, :, :], wide(stat[2][:, :]), ALU.mult).then_inc(y_ready, 1)

            def row5(r):
                n = all_before(r)
                count = SEEN0[5] + n + r + 1
                if isinstance(r, int) and r < 3:
                    fix_diag(5, None, count)
                    if r == 0:
                        with dve.If(flag < 1):
                            step(V.memset, X[:, :, 0:D], 0.0)
                            dve.drain()
                        dve.drain()
                    else:
                        softmax(r - 1)
                else:
                    softmax(r - 1)
                    if not isinstance(r, int):
                        candidates(r - 1)
                        cells(r - 1)
                    fix_diag(5, None, count)
                if isinstance(r, int) and r > 0:
                    candidates(r - 1)
                end_row(r)
                if isinstance(r, int) and r > 0:
                    cells(r - 1)
                if not (isinstance(r, int) and r == 0):
                    last_norm(r - 1)
            for_rows(dve, row5, 5)
            softmax(ROWS - 1)
            candidates(ROWS - 1)
            cells(ROWS - 1)
            last_norm(ROWS - 1)


WEIGHT_LOADS = 38


def kernel(**inputs):
    import numpy as np
    import concourse.bacc as bacc
    from concourse.bass_utils import run_bass_kernel_spmd

    a = {k: np.asarray(val) for k, val in inputs.items()}
    adj = a["adj"].reshape(ROWS, SB, ROWS, Q, KK, P).transpose(0, 2, 3, 5, 4, 1)
    arrays = {
        "adj_t": np.ascontiguousarray(adj).reshape(ROWS * ROWS * Q, P, KK * SB),
        "x": np.ascontiguousarray(a["x"].reshape(TILES, P, D).transpose(1, 0, 2)).reshape(P, TILES * D),
        "w0": np.ascontiguousarray(a["L0_gnn_W"]),
        "w2t": np.ascontiguousarray(a["L2_gnn_W_weight"].T),
        "b2": np.ascontiguousarray(a["L2_gnn_W_bias"]),
        "wg": np.ascontiguousarray(a["L3_gnn_W_gat"]),
        "wgt": np.ascontiguousarray(a["L3_gnn_W_gat"].T),
        "a_gat": np.ascontiguousarray(a["L3_gnn_a_gat"]),
    }
    for c in "en":
        arrays[f"wih{c}"] = np.ascontiguousarray(a[f"L3_gnn_w_ih_{c}"].T)
        arrays[f"whh{c}"] = np.ascontiguousarray(a[f"L3_gnn_w_hh_{c}"].T)
        arrays[f"bih{c}"] = np.ascontiguousarray(a[f"L3_gnn_b_ih_{c}"]).reshape(1, 3 * D)
        arrays[f"bhh{c}"] = np.ascontiguousarray(a[f"L3_gnn_b_hh_{c}"]).reshape(1, 3 * D)
    order = ["adj_t", "x", "w0", "w2t", "b2", "wg", "wgt", "a_gat",
             "wihe", "whhe", "bihe", "bhhe", "wihn", "whhn", "bihn", "bhhn"]

    nc = bacc.Bacc("TRN2", target_bir_lowering=False, num_devices=1)
    args = [nc.dram_tensor(f"in_{n}", arrays[n].shape, mybir.dt.from_np(arrays[n].dtype), kind="ExternalInput").ap()
            for n in order]
    args.append(nc.dram_tensor("out_y", (P, TILES * D), F32, kind="ExternalOutput").ap())
    build(nc, *args)
    r = run_bass_kernel_spmd(nc, [{f"in_{n}": arrays[n] for n in order}], core_ids=[0])
    got = r.results[0]["out_y"]
    return np.ascontiguousarray(got.reshape(P, TILES, D).transpose(1, 0, 2)).reshape(N, D)
```
